# Optimizing a Trainium2 kernel written in Bass

```python
import numpy as np
import jax
import jax.numpy as jnp

def _softmax(x, axis=-1):
    return jax.nn.softmax(x, axis=axis)

def _gelu(x):
    return jax.nn.gelu(x, approximate=True)

def _silu(x):
    return jax.nn.silu(x)

def _sigmoid(x):
    return jax.nn.sigmoid(x)

def _layernorm(x, axis=-1, eps=1e-05):
    m = jnp.mean(x, axis=axis, keepdims=True)
    v = jnp.var(x, axis=axis, keepdims=True)
    return (x - m) / jnp.sqrt(v + eps)

def _scatter_add(tgt, idx, src, axis=0):
    return tgt.at[idx].add(src)

def _segment_sum(src, seg, n):
    return jax.ops.segment_sum(src, seg, n)
kernel_name = 'mk_decoder_postln_d1_seqx_r8_446aa3'

def setup_inputs(seed: int=0):
    np.random.seed(seed)
    _w = jnp.asarray

    def _rec_inputs():
        import jax
        import jax.numpy as jnp
        _rk = jax.random.key(seed)
        x = 0.002226 + 0.9996 * jax.random.normal(jax.random.fold_in(_rk, 1), (8, 256, 128), jnp.float32)
        _lenS = 256 - jax.random.randint(jax.random.fold_in(_rk, 7), (8,), 0, max(1, 256 // 4) + 1, jnp.int32)
        _lenS2 = 512 - jax.random.randint(jax.random.fold_in(_rk, 8), (8,), 0, max(1, 512 // 4) + 1, jnp.int32)
        _ctx_1024P = jax.random.normal(jax.random.fold_in(_rk, 11), (8, 16, 128), jnp.float32)
        _ctx_1024c = jax.random.dirichlet(jax.random.fold_in(_rk, 511), 0.3 * jnp.ones((16,), jnp.float32), (8, 512))
        _ctx_1024t = jnp.einsum('bsk,bkd->bsd', _ctx_1024c, _ctx_1024P)
        _ctx_1024t = _ctx_1024t * jax.lax.rsqrt(jnp.mean(jnp.square(_ctx_1024t)) + 1e-12) * 0.953939
        ctx_1024 = -0.000125008 + 0.999885 * (_ctx_1024t + 0.3 * jax.random.normal(jax.random.fold_in(_rk, 611), (8, 512, 128), jnp.float32))
        _validS = jnp.arange(256)[None, :] < _lenS[:, None]
        _validS2 = jnp.arange(512)[None, :] < _lenS2[:, None]
        _causal = jnp.tril(jnp.ones((256, 256), dtype=bool))
        mask_BxS2_bk0 = jnp.logical_not(jnp.broadcast_to(_validS2[:, :], (8, 512)))
        return (x, ctx_1024, mask_BxS2_bk0)
    x, ctx_1024, mask_BxS2_bk0 = _rec_inputs()

    def _L0_attn_setup():
        import jax, jax.numpy as jnp
        import numpy as np
        key = jax.random.key(seed)
        ks = jax.random.split(key, 5)
        B, S, D = (2, 256, 128)
        scale = 0.02
        return {'x': jax.random.normal(ks[0], (B, S, D), dtype=jnp.float32), 'q_proj_weight': jax.random.normal(ks[1], (D, D), dtype=jnp.float32) * scale, 'k_proj_weight': jax.random.normal(ks[2], (D, D), dtype=jnp.float32) * scale, 'v_proj_weight': jax.random.normal(ks[3], (D, D), dtype=jnp.float32) * scale, 'o_proj_weight': jax.random.normal(ks[4], (D, D), dtype=jnp.float32) * scale}
    _L0_attn_all = _L0_attn_setup()
    _L0_attn_in = {k: v for k, v in _L0_attn_all.items() if k in ('q_proj_weight', 'k_proj_weight', 'v_proj_weight', 'o_proj_weight')}
    del _L0_attn_all

    def _L0_xattn_setup():
        import jax, jax.numpy as jnp
        import numpy as np
        EPS = 1e-05

        def layer_norm(x, g, b):
            mu = jnp.mean(x, axis=-1, keepdims=True)
            var = jnp.mean((x - mu) ** 2, axis=-1, keepdims=True)
            return (x - mu) * jax.lax.rsqrt(var + EPS) * g + b
        key = jax.random.key(seed)
        ks = jax.random.split(key, 8)
        b, n, l, D = (8, 512, 64, 128)
        heads, dim_head = (16, 64)
        inner = heads * dim_head
        x = jax.random.normal(ks[0], (b, n, D), dtype=jnp.float32)
        latents = jax.random.normal(ks[1], (b, l, D), dtype=jnp.float32)
        mask = jax.random.randint(ks[2], (b, n), 0, 2) > 0
        Wq = jax.random.normal(ks[3], (D, inner), dtype=jnp.float32) * D ** (-0.5)
        Wkv = jax.random.normal(ks[4], (D, 2 * inner), dtype=jnp.float32) * D ** (-0.5)
        Wout = jax.random.normal(ks[5], (inner, D), dtype=jnp.float32) * inner ** (-0.5)
        g1 = jnp.ones((D,), jnp.float32)
        b1 = jnp.zeros((D,), jnp.float32)
        g2 = jnp.ones((D,), jnp.float32)
        b2 = jnp.zeros((D,), jnp.float32)
        return {'x': x, 'latents': latents, 'mask': mask, 'g1': g1, 'b1': b1, 'g2': g2, 'b2': b2, 'Wq': Wq, 'Wkv': Wkv, 'Wout': Wout}
    _L0_xattn_all = _L0_xattn_setup()
    _L0_xattn_in = {k: v for k, v in _L0_xattn_all.items() if k in ('g1', 'b1', 'g2', 'b2', 'Wq', 'Wkv', 'Wout')}
    del _L0_xattn_all

    def _L0_ffn_setup():
        import jax, jax.numpy as jnp
        import numpy as np
        D_MODEL = 128
        HIDDEN = 256
        N_EXPERTS = 8
        TOP_K = 2
        BATCH = 2
        SEQ = 256
        key = jax.random.key(seed)
        ks = jax.random.split(key, 9)
        s = 0.02
        return {'x': jax.random.normal(ks[0], (BATCH, SEQ, D_MODEL), dtype=jnp.float32), 'w_router': jax.random.normal(ks[1], (D_MODEL, N_EXPERTS), dtype=jnp.float32) * s, 'w1': jax.random.normal(ks[2], (N_EXPERTS, D_MODEL, HIDDEN), dtype=jnp.float32) * s, 'w3': jax.random.normal(ks[3], (N_EXPERTS, D_MODEL, HIDDEN), dtype=jnp.float32) * s, 'w2': jax.random.normal(ks[4], (N_EXPERTS, HIDDEN, D_MODEL), dtype=jnp.float32) * s, 'sw1': jax.random.normal(ks[5], (D_MODEL, HIDDEN), dtype=jnp.float32) * s, 'sw3': jax.random.normal(ks[6], (D_MODEL, HIDDEN), dtype=jnp.float32) * s, 'sw2': jax.random.normal(ks[7], (HIDDEN, D_MODEL), dtype=jnp.float32) * s}
    _L0_ffn_all = _L0_ffn_setup()
    _L0_ffn_in = {k: v for k, v in _L0_ffn_all.items() if k in ('w_router', 'w1', 'w3', 'w2', 'sw1', 'sw3', 'sw2')}
    del _L0_ffn_all
    return {'x': x, 'ctx_1024': ctx_1024, 'mask_BxS2_bk0': mask_BxS2_bk0, 'L0_attn_q_proj_weight': _L0_attn_in['q_proj_weight'], 'L0_attn_k_proj_weight': _L0_attn_in['k_proj_weight'], 'L0_attn_v_proj_weight': _L0_attn_in['v_proj_weight'], 'L0_attn_o_proj_weight': _L0_attn_in['o_proj_weight'], 'L0_xattn_g1': _L0_xattn_in['g1'], 'L0_xattn_b1': _L0_xattn_in['b1'], 'L0_xattn_g2': _L0_xattn_in['g2'], 'L0_xattn_b2': _L0_xattn_in['b2'], 'L0_xattn_Wq': _L0_xattn_in['Wq'], 'L0_xattn_Wkv': _L0_xattn_in['Wkv'], 'L0_xattn_Wout': _L0_xattn_in['Wout'], 'L0_ffn_w_router': _L0_ffn_in['w_router'], 'L0_ffn_w1': _L0_ffn_in['w1'], 'L0_ffn_w3': _L0_ffn_in['w3'], 'L0_ffn_w2': _L0_ffn_in['w2'], 'L0_ffn_sw1': _L0_ffn_in['sw1'], 'L0_ffn_sw3': _L0_ffn_in['sw3'], 'L0_ffn_sw2': _L0_ffn_in['sw2']}

def reference(x, ctx_1024, mask_BxS2_bk0, L0_attn_q_proj_weight, L0_attn_k_proj_weight, L0_attn_v_proj_weight, L0_attn_o_proj_weight, L0_xattn_g1, L0_xattn_b1, L0_xattn_g2, L0_xattn_b2, L0_xattn_Wq, L0_xattn_Wkv, L0_xattn_Wout, L0_ffn_w_router, L0_ffn_w1, L0_ffn_w3, L0_ffn_w2, L0_ffn_sw1, L0_ffn_sw3, L0_ffn_sw2):
    import jax
    import jax.numpy as jnp

    def _L0_attn_ref(x, q_proj_weight, k_proj_weight, v_proj_weight, o_proj_weight):
        import jax, jax.numpy as jnp
        import numpy as np
        num_heads = 16
        B, S, d_in = x.shape
        d_k = q_proj_weight.shape[0]
        head_size = d_k // num_heads

        def split_heads(t):
            return t.reshape(B, S, num_heads, head_size).transpose(0, 2, 1, 3)
        q = split_heads(jnp.einsum('bsd,kd->bsk', x, q_proj_weight))
        k = split_heads(jnp.einsum('bsd,kd->bsk', x, k_proj_weight))
        v = split_heads(jnp.einsum('bsd,kd->bsk', x, v_proj_weight))
        scale = jnp.float32(head_size) ** (-0.5)
        scores = jnp.einsum('bhtc,bhkc->bhtk', q, k) * scale
        causal = jnp.tril(jnp.ones((S, S), dtype=bool))
        scores = jnp.where(causal, scores, -jnp.inf)
        attn = jax.nn.softmax(scores, axis=-1)
        out = jnp.einsum('bhtk,bhkc->bhtc', attn, v)
        out = out.transpose(0, 2, 1, 3).reshape(B, S, d_k)
        return jnp.einsum('bsv,dv->bsd', out, o_proj_weight)

    def _L0_xattn_ref(x, latents, mask, g1, b1, g2, b2, Wq, Wkv, Wout):
        import jax, jax.numpy as jnp
        import numpy as np
        EPS = 1e-05

        def layer_norm(x, g, b):
            mu = jnp.mean(x, axis=-1, keepdims=True)
            var = jnp.mean((x - mu) ** 2, axis=-1, keepdims=True)
            return (x - mu) * jax.lax.rsqrt(var + EPS) * g + b
        heads, dim_head = (16, 64)
        b, n, D = x.shape
        l = latents.shape[1]
        xn = layer_norm(x, g1, b1)
        ln_lat = layer_norm(latents, g2, b2)
        q = ln_lat @ Wq
        kv = jnp.concatenate([xn, ln_lat], axis=1) @ Wkv
        k, v = jnp.split(kv, 2, axis=-1)

        def to_heads(t):
            return t.reshape(t.shape[0], t.shape[1], heads, dim_head).transpose(0, 2, 1, 3)
        q, k, v = (to_heads(q), to_heads(k), to_heads(v))
        scale = 1.0 / np.sqrt(np.sqrt(dim_head)).astype(np.float32)
        weight = jnp.einsum('bhld,bhnd->bhln', q * scale, k * scale)
        full_mask = jnp.concatenate([mask, jnp.ones((b, l), dtype=bool)], axis=1)
        neg = -jnp.finfo(weight.dtype).max
        weight = jnp.where(full_mask[:, None, None, :], weight, neg)
        weight = jax.nn.softmax(weight.astype(jnp.float32), axis=-1).astype(q.dtype)
        out = jnp.einsum('bhln,bhnd->bhld', weight, v)
        out = out.transpose(0, 2, 1, 3).reshape(b, l, heads * dim_head)
        return out @ Wout

    def _L0_ffn_ref(x, w_router, w1, w3, w2, sw1, sw3, sw2):
        import jax, jax.numpy as jnp
        import numpy as np
        D_MODEL = 128
        HIDDEN = 256
        N_EXPERTS = 8
        TOP_K = 2
        BATCH = 2
        SEQ = 256
        b, s, d = x.shape
        xf = x.reshape(b * s, d)
        probs = jax.nn.softmax(xf @ w_router, axis=-1)
        top_vals, top_idx = jax.lax.top_k(probs, TOP_K)
        gates = top_vals / jnp.sum(top_vals, axis=-1, keepdims=True)
        onehot = jax.nn.one_hot(top_idx, N_EXPERTS, dtype=xf.dtype)
        cw = jnp.einsum('tk,tke->te', gates, onehot)
        h1 = jnp.einsum('td,edh->eth', xf, w1)
        h3 = jnp.einsum('td,edh->eth', xf, w3)
        y = jnp.einsum('eth,ehd->etd', jax.nn.silu(h1) * h3, w2)
        out = jnp.einsum('etd,te->td', y, cw)
        out = out + jax.nn.silu(xf @ sw1) * (xf @ sw3) @ sw2
        return out.reshape(b, s, d)
    x = _layernorm(x + _L0_attn_ref(x, L0_attn_q_proj_weight, L0_attn_k_proj_weight, L0_attn_v_proj_weight, L0_attn_o_proj_weight), axis=-1)
    x = _layernorm(x + _L0_xattn_ref(ctx_1024, x, mask_BxS2_bk0, L0_xattn_g1, L0_xattn_b1, L0_xattn_g2, L0_xattn_b2, L0_xattn_Wq, L0_xattn_Wkv, L0_xattn_Wout), axis=-1)
    x = _layernorm(x + _L0_ffn_ref(x, L0_ffn_w_router, L0_ffn_w1, L0_ffn_w3, L0_ffn_w2, L0_ffn_sw1, L0_ffn_sw3, L0_ffn_sw2), axis=-1)
    return x

_drawn_inputs = setup_inputs


def setup_inputs(seed=0):
    import zlib

    import numpy as np

    out = dict(_drawn_inputs(seed))
    spreads = {'L0_xattn_g1': (1.0, 0.2),
     'L0_xattn_b1': (0.0, 0.395),
     'L0_xattn_g2': (1.0, 0.2),
     'L0_xattn_b2': (0.0, 0.1)}
    factors = {'L0_attn_q_proj_weight': 8.0,
     'L0_attn_k_proj_weight': 8.0,
     'L0_attn_v_proj_weight': 6.344,
     'L0_attn_o_proj_weight': 6.325,
     'L0_ffn_w_router': 8.0,
     'L0_ffn_w1': 8.0,
     'L0_ffn_w3': 8.0,
     'L0_ffn_w2': 8.0,
     'L0_ffn_sw1': 6.966,
     'L0_ffn_sw3': 6.878,
     'L0_ffn_sw2': 6.878}
    for name, (base, spread) in spreads.items():
        noise = np.random.default_rng([zlib.crc32(name.encode()), seed]).standard_normal(out[name].shape)
        drawn = base * np.exp(spread * noise) if base else spread * noise
        out[name] = jnp.asarray(drawn.astype(out[name].dtype))
    for name, factor in factors.items():
        out[name] = (out[name] * factor).astype(out[name].dtype)
    return out
```

```python
from contextlib import ExitStack

import concourse.bass as bass
from concourse import mybir

ALU = mybir.AluOpType
ACT = mybir.ActivationFunctionType
AX = mybir.AxisListType
F32 = mybir.dt.float32
F32R = mybir.dt.float32r
U8 = mybir.dt.uint8
U32 = mybir.dt.uint32

P = 128
BANK = 512
SLOTS = 3
O_BANK = 2 * SLOTS
BIG = 1e30
EPS = 1e-5


class Shared:
    pass


class Window:

    def __init__(self, batch, steps, jobs, start, previous, parity=0):
        self.batch, self.steps, self.parity = batch, steps, parity
        mine = [s for s in steps if s[0] in jobs]
        both = [(k, r - 1, i) for k, r, i in previous if k in jobs] + mine
        self.slot, self.before = {}, {}
        for n, key in enumerate(mine):
            self.slot[key] = (start + n) % SLOTS
            at = len(both) - len(mine) + n - SLOTS
            self.before[key] = both[at] if at >= 0 else None
        self.count = len(mine)

    def moved(self, batch):
        w = Window(batch, self.steps, (), 0, (), self.parity)
        w.slot, w.before = self.slot, self.before
        return w


def plan_windows(batches, steps_of, jobs, unroll):
    def kept(b):
        return [s for s in steps_of if 0 <= b + s[1] < batches]
    windows, start, previous = [], 0, []
    for b in range(-1, batches + 1):
        w = Window(b, kept(b), jobs, start, previous, parity=b % 2)
        windows.append(w)
        start, previous = start + w.count, w.steps
    first, last = windows[1], windows[batches]
    looped = windows[2:2 + unroll]
    assert (batches - 2) % unroll == 0 and (unroll * looped[0].count) % SLOTS == 0
    for n, w in enumerate(windows[2:batches]):
        assert w.slot == looped[n % unroll].slot and w.before == looped[n % unroll].before
    return windows[0], first, looped, last, windows[batches + 1]


def run_windows(engine, plan, batches, emit):
    prologue, first, looped, last, tail = plan
    emit(prologue)
    emit(first)
    with engine.Fori(0, (batches - 2) // len(looped)) as turn:
        for n, w in enumerate(looped):
            emit(w.moved(turn * len(looped) + 1 + n))
    emit(last)
    emit(tail)


def hold(dve, place):
    dve.memset(place, 0.0)


def wait(engine, semaphore, count):
    if not isinstance(count, int) or count > 0:
        engine.wait_ge(semaphore, count)


def decoder_layer(nc, x, ctx, mask, wq, wk, wv, wo, g1, b1, g2, b2, xwq, xwkv, xwout,
                  w_router, w1, w3, w2, sw1, sw3, sw2, out):
    B, S, D = x.shape
    C = ctx.shape[1]
    T = S // P
    CT = C // P
    KT = CT + T
    KEYS = C + S
    SH = 16
    SD = D // SH
    SG = 4
    XH = 16
    XD = xwq.shape[1] // XH
    PAIRS = XH // 2
    INNER = XH * XD
    E, _, HID = w1.shape
    HB = HID // P
    NE = E + 1
    assert D == P and XD == 64 and SD == 8 and S == 2 * P and HB == 2

    top = ExitStack()

    def sem(name):
        return top.enter_context(nc.semaphore(name))

    def sb(stack, name, shape, dt=F32):
        return stack.enter_context(nc.sbuf_tensor(name, shape, dt))

    with top:
        ps = top.enter_context(nc.psum_tensor("ps", [P, 8, BANK], F32))

        def slot(s, n=2 * BANK, at=0):
            return ps[:, 2 * s:2 * s + 2, :].rearrange("p a b -> p (a b)")[:, at:at + n]

        ident = sb(top, "ident", [P, P])
        ones = sb(top, "ones", [P, S])
        state = sb(top, "state", [P, B * T, D])
        stats = sb(top, "stats", [P, B * KT, 6])
        mean = sb(top, "mean", [P, B * KT])
        rstd = sb(top, "rstd", [P, B * KT])
        var = sb(top, "var", [P, B * KT])
        tmp = sb(top, "tmp", [P, B * KT])
        gb = sb(top, "gb", [P, 4])
        w_rt = sb(top, "w_rt", [P, E])

        cross = ExitStack()
        top.enter_context(cross)
        ctx_all = sb(cross, "ctx_all", [P, B * CT, D])
        keep_all = sb(cross, "keep_all", [P, B, C // 4], U32)
        wk_hi = sb(cross, "wk_hi", [P, INNER], F32R)
        wk_lo = sb(cross, "wk_lo", [P, INNER], F32R)
        wv_hi = sb(cross, "wv_hi", [P, INNER], F32R)
        wv_lo = sb(cross, "wv_lo", [P, INNER], F32R)
        wq_hi = sb(cross, "wq_hi", [P, XH, 2, XD], F32R)
        wq_lo = sb(cross, "wq_lo", [P, XH, 2, XD], F32R)
        wout = sb(cross, "wout", [P, PAIRS, D])

        m = Shared()
        m.x, m.ctx, m.mask, m.wq, m.wk, m.wv = x, ctx, mask, wq, wk, wv
        m.wo, m.g1, m.b1, m.g2, m.b2, m.xwq = wo, g1, b1, g2, b2, xwq
        m.xwkv, m.xwout, m.w_router, m.w1, m.w3, m.w2 = xwkv, xwout, w_router, w1, w3, w2
        m.sw1, m.sw3, m.sw2, m.B, m.S, m.D = sw1, sw3, sw2, B, S, D
        m.T, m.C, m.CT, m.KT, m.KEYS, m.SH = T, C, CT, KT, KEYS, SH
        m.SD, m.SG, m.XH, m.XD, m.PAIRS, m.INNER = SD, SG, XH, XD, PAIRS, INNER
        m.E, m.NE, m.HID, m.HB, m.ident, m.ones = E, NE, HID, HB, ident, ones
        m.state, m.stats, m.mean, m.rstd, m.gb, m.w_rt = state, stats, mean, rstd, gb, w_rt
        m.ctx_all, m.keep_all, m.wk_hi, m.wk_lo, m.wv_hi, m.wv_lo = ctx_all, keep_all, wk_hi, wk_lo, wv_hi, wv_lo
        m.wq_hi, m.wq_lo, m.wout = wq_hi, wq_lo, wout

        self_attention(nc, sem, sb, ps, slot, m)
        normalize(nc, sem, "n1", B * T, state, stats, mean, rstd, var, tmp, T, CT, KT, whole=True, again=True)
        cross_attention(nc, sem, sb, ps, slot, m)
        normalize(nc, sem, "n2", B * T, state, stats, mean, rstd, var, tmp, T, CT, KT)
        cross.close()
        experts(nc, sem, sb, ps, slot, m)
        normalize(nc, sem, "n3", B * T, state, stats, mean, rstd, var, tmp, T, CT, KT, out=out)


def normalize(nc, sem, name, tiles, state, stats, mean, rstd, var, tmp, T, CT, KT,
              whole=False, again=False, out=None):
    chain = sem(name + "_chain")
    var_ready = sem(name + "_var_ready")
    std_ready = sem(name + "_std_ready")
    stored = sem(name + "_stored")
    rows = stats[:, :, :].rearrange("p (b k) s -> p b k s", k=KT)
    n_batch = tiles // T

    def per_tile(a, everything):
        v = a[:, :].rearrange("p (b k) -> p b k", k=KT)
        return v if everything else v[:, :, CT:KT]

    rounds = [whole] + [False] * again
    with nc.Block() as block:

        @block.vector
        def _(dve):
            count = [0]

            def link(instruction):
                count[0] += 1
                instruction.then_inc(chain, 1)
                dve.wait_ge(chain, count[0])

            def moments(everything):
                st = rows if everything else rows[:, :, CT:KT, :]
                me, ve, mo, vo = (st[:, :, :, i] for i in (1, 2, 4, 5))
                m, v, t = (per_tile(a, everything) for a in (mean, var, tmp))
                link(dve.tensor_tensor(t, me, mo, ALU.subtract))
                link(dve.tensor_tensor(t, t, t, ALU.mult))
                link(dve.tensor_tensor(v, ve, vo, ALU.add))
                link(dve.tensor_scalar(v, v, 1.0 / P, EPS, ALU.mult, ALU.add))
                link(dve.tensor_scalar(t, t, 0.25, None, ALU.mult))
                link(dve.tensor_tensor(m, me, mo, ALU.add))
                link(dve.tensor_scalar(m, m, 0.5, None, ALU.mult))
                dve.tensor_tensor(v, v, t, ALU.add).then_inc(var_ready, 1)

            def reciprocal_root(n, everything):
                v, t, r = (per_tile(a, everything) for a in (var, tmp, rstd))
                dve.wait_ge(std_ready, n)
                link(dve.reciprocal(r, r))
                link(dve.tensor_tensor(t, r, r, ALU.mult))
                link(dve.tensor_tensor(t, t, v, ALU.mult))
                link(dve.tensor_scalar(t, t, -0.5, 1.5, ALU.mult, ALU.add))
                link(dve.tensor_tensor(r, r, t, ALU.mult))

            def tile_norm(i):
                at = (i // T) * KT + CT + i % T
                return dve.tensor_scalar(state[:, i, :], state[:, i, :], mean[:, at:at + 1],
                                         rstd[:, at:at + 1], ALU.subtract, ALU.mult)

            for n, everything in enumerate(rounds):
                moments(everything)
                reciprocal_root(n + 1, everything)
                if n == 0:
                    for i in range(tiles):
                        last = tile_norm(i)
                        if out is not None or i == tiles - 1:
                            last.then_inc(chain, 1)
                            count[0] += 1
                    dve.wait_ge(chain, count[0])
                    if again:
                        for i in range(tiles):
                            at = (i // T) * KT + CT + i % T
                            last = dve.bn_stats(stats[:, at, :], state[:, i, :])
                        link(last)

        @block.scalar
        def _(act):
            for n, everything in enumerate(rounds):
                act.wait_ge(var_ready, n + 1)
                nc.scalar.activation(per_tile(rstd, everything), per_tile(var, everything),
                                     ACT.Sqrt).then_inc(std_ready, 1)

        if out is not None:
            @block.sync
            def _(sp):
                rows_out = out.rearrange("b (j p) d -> p (b j) d", p=P)
                step = 2 * T
                for i in range(0, tiles, step):
                    sp.wait_ge(chain, 12 + i + step)
                    sp.dma_start(rows_out[:, i:i + step, :], state[:, i:i + step, :]).then_inc(stored, 16)
                sp.wait_ge(stored, 16 * (tiles // step))


def self_attention(nc, sem, sb, ps, slot, m):
    B, S, D, T, C, CT, KT = m.B, m.S, m.D, m.T, m.C, m.CT, m.KT
    SH, SD, SG, XH, INNER = m.SH, m.SD, m.SG, m.XH, m.INNER
    ident, state, stats, gb = m.ident, m.state, m.stats, m.gb
    ctx_all, keep_all, wout, w_rt = m.ctx_all, m.keep_all, m.wout, m.w_rt
    SCALE = float(SD) ** -0.5
    HG = SH // SG
    QROWS = P // HG
    PV_COLS = 3 * P
    RING = 8

    mem = ExitStack()
    x_in = sb(mem, "x_in", [P, 2, T, D])
    raw = sb(mem, "raw", [P, 4, D])
    wt = sb(mem, "wt", [P, 3, D])
    wt_hi = sb(mem, "wt_hi", [P, 3, D], F32R)
    wt_lo = sb(mem, "wt_lo", [P, 3, D])
    aq_hi, aq_lo, ak_hi, ak_lo = (
        sb(mem, n, [P, SG, 4, 32], F32R) for n in ("aq_hi", "aq_lo", "ak_hi", "ak_lo"))
    av_hi = sb(mem, "av_hi", [P, SH, 32], F32R)
    av_lo = sb(mem, "av_lo", [P, SH, 32], F32R)
    wo_pad = sb(mem, "wo_pad", [P, SH, 32])
    wo_t = sb(mem, "wo_t", [P, SG, D])
    part = sb(mem, "part", [P, 2])
    head_of = sb(mem, "head_of", [P, HG])
    causal = sb(mem, "causal", [P, S])
    xt_hi = sb(mem, "xt_hi", [P, 2, S], F32R)
    xt_lo = sb(mem, "xt_lo", [P, 2, S], F32R)
    round_kq = sb(mem, "round_kq", [P, 2, S], F32R)
    k_parts = sb(mem, "k_parts", [P, SG, S], F32R)
    q_parts = sb(mem, "q_parts", [P, 2, S], F32R)
    q_head = sb(mem, "q_head", [P, 4, S], F32R)
    vals = sb(mem, "vals", [P, 2, T, SH, 32])
    masked = sb(mem, "masked", [P, 2, PV_COLS])
    spare = sb(mem, "spare", [P, 2])
    low = sb(mem, "low", [P, 2, T])
    probs = sb(mem, "probs", [P, 4, PV_COLS])
    sums = sb(mem, "sums", [P, 2, T, HG])
    rsum = sb(mem, "rsum", [P, 2, T, HG])
    rsum_wide = sb(mem, "rsum_wide", [P, 2, T, HG, 32])
    rsum_t = sb(mem, "rsum_t", [P, 2, S])
    probs_t = sb(mem, "probs_t", [P, RING, PV_COLS])
    heads_t = sb(mem, "heads_t", [P, SG, S])
    raw_kv = sb(mem, "raw_kv", [P, 2 * INNER])
    raw_q = sb(mem, "raw_q", [P, INNER])

    loaded_w, loaded_x, loaded_b = sem("a_loaded_w"), sem("a_loaded_x"), sem("a_loaded_b")
    loaded_kv, loaded_rest = sem("a_loaded_kv"), sem("a_loaded_rest")
    consts = sem("a_consts")
    wt_full = sem("a_wt_full")
    wt_out = sem("a_wt_out")
    setup = sem("a_setup")
    weights = sem("a_weights")
    cross_hi = sem("a_cross_hi")
    cross_lo = sem("a_cross_lo")
    full = {k: sem(f"a_{k}_full") for k in ("T", "KQ", "V", "S", "PT", "R", "OUT")}
    xh_done, x_ready = sem("a_xh_done"), sem("a_x_ready")
    round_done, kq_ready = sem("a_round_done"), sem("a_kq_ready")
    qh_ready = sem("a_qh_ready")
    v_ready = sem("a_v_ready")
    masked_ready = sem("a_masked_ready")
    exp_done = sem("a_exp_done")
    pt_act, pt_dve = sem("a_pt_act"), sem("a_pt_dve")
    rsum_ready = sem("a_rsum_ready")
    wide_ready = sem("a_wide_ready")
    rsum_t_ready = sem("a_rsum_t_ready")
    pv_done = sem("a_pv_done")
    heads_ready = sem("a_heads_ready")
    added = sem("a_added")
    measured = sem("a_measured")

    jobs = {"T", "KQ", "V", "S", "PT", "R", "OUT"}

    def taken(kind, batch, i):
        if kind == "PT":
            return (pt_dve if i % 2 else pt_act), batch * (SH // 2) + i // 2 + 1
        semaphore, per, extra = {
            "T": (x_ready, T, 1), "KQ": (kq_ready, 2 * SG, 2), "V": (v_ready, 1, 1),
            "S": (masked_ready, SH * T, T), "R": (rsum_t_ready, SG, 1), "OUT": (added, T, 1)}[kind]
        return semaphore, batch * per + i * extra + extra

    steps = []
    for t in range(SH):
        steps.append(("S", 0, t))
        late = t - 2
        steps.append(("PT", late // SH, late % SH))
        steps.append(("EXP", 0, t))
        if t % HG == 1:
            nxt = t // HG + 1
            steps.append(("KQ", nxt // SG, nxt % SG))
        if t % HG == 2:
            g = (t - 6) // HG
            steps.append(("R", g // SG, g % SG))
        if t % HG == 3:
            g = (t - 7) // HG
            steps.append(("PV", g // SG, g % SG))
        if t % HG == 0:
            g = (t - 8) // HG
            steps.append(("NORM", g // SG, g % SG))
        nxt = t + 2
        steps.append(("QH", nxt // SH, nxt % SH))
        if t == 5:
            steps += [("OUT", -1, 0), ("OUT", -1, 1)]
        if t == 8:
            steps += [("T", 1, 0), ("T", 1, 1)]
        if t == 10:
            steps.append(("V", 1, 0))
    plan = plan_windows(B, steps, jobs, 2)

    x_rows = m.x.rearrange("b (j p) d -> b p j d", p=P)

    with nc.Block() as block:

        @block.sync
        def _(sp):
            for i, w in enumerate((m.wq, m.wk, m.wv, m.wo)):
                sp.dma_start(raw[:, i, :], w).then_inc(loaded_w, 16)

            def emit(w):
                for kind, rel, i in w.steps:
                    if kind == "T" and i == 0:
                        b = w.batch + rel
                        wait(sp, added, (b - 1) * T)
                        wait(sp, loaded_x, 16 * b)
                        sp.dma_start(x_in[:, (w.parity + rel) % 2, :, :], x_rows[b]).then_inc(loaded_x, 16)
            run_windows(sp, plan, B, emit)
            sp.wait_ge(loaded_rest, 16 * 7)

        @block.gpsimd
        def _(pool):
            pool.memset(ident[:, :], 0.0).then_inc(consts, 1)
            pool.memset(causal[:, :], 0.0).then_inc(consts, 1)
            pool.memset(m.ones[:, :], 1.0).then_inc(consts, 1)
            pool.wait_ge(consts, 3)
            pool.affine_select(out=ident[:, :], in_=ident[:, :], compare_op=ALU.not_equal, fill=1.0,
                               base=0, pattern=[[-1, P]], channel_multiplier=1).then_inc(consts, 1)
            pool.affine_select(out=causal[:, P:S], in_=causal[:, P:S], compare_op=ALU.is_ge, fill=BIG,
                               base=0, pattern=[[-1, P]], channel_multiplier=1).then_inc(consts, 1)
            dst = ((m.wk_lo[:, :], raw_kv[:, 0:INNER], m.wk_hi[:, :]),
                   (m.wv_lo[:, :], raw_kv[:, INNER:2 * INNER], m.wv_hi[:, :]))
            for i, (lo, whole, hi) in enumerate(dst):
                pool.wait_ge(cross_hi, i + 1)
                pool.tensor_tensor(lo, whole, hi.bitcast(F32), ALU.subtract).then_inc(cross_lo, 1)
            pool.wait_ge(cross_hi, 4)
            for r in range(2):
                pool.tensor_tensor(m.wq_lo[:, :, r, :], raw_q[:, :].rearrange("p (h c) -> p h c", h=XH),
                                   m.wq_hi[:, :, r, :].bitcast(F32), ALU.subtract).then_inc(cross_lo, 1)

            def emit(w):
                for kind, rel, i in w.steps:
                    if kind == "R":
                        n = (w.batch + rel) * SG + i
                        pool.wait_ge(rsum_ready, n + 1)
                        src = rsum[:, i % 2, :, :].rearrange("p t h -> p (t h)").unsqueeze(2)
                        pool.tensor_tensor(rsum_wide[:, i % 2, :, :, :].rearrange("p t h c -> p (t h) c"),
                                           m.ones[:, :].rearrange("p (a c) -> p a c", c=32),
                                           src.broadcast_to([P, T * HG, 32]), ALU.mult).then_inc(wide_ready, 1)
            run_windows(pool, plan, B, emit)

        @block.scalar
        def _(act):
            for w_in, o in ((m.xwkv, raw_kv[:, :]), (m.xwq, raw_q[:, :])):
                act.dma_start(o, w_in).then_inc(loaded_kv, 16)
            for n, w_in in enumerate((m.g1, m.b1, m.g2, m.b2)):
                act.dma_start(gb[:, n:n + 1], w_in.rearrange("(p o) -> p o", o=1)).then_inc(loaded_rest, 16)
            act.dma_start(ctx_all[:, :, :], m.ctx.rearrange("b (j p) d -> p (b j) d", p=P)).then_inc(loaded_b, 16)
            act.dma_start(keep_all[:, :, :], m.mask.rearrange("b c -> (b c)").partition_broadcast(P)
                          .rearrange("p (b c) -> p b c", b=B)).then_inc(loaded_rest, 16)
            act.dma_start(wout[:, :, :], m.xwout.rearrange("(r p) d -> p r d", p=P)).then_inc(loaded_rest, 16)
            act.dma_start(w_rt[:, :], m.w_router).then_inc(loaded_rest, 16)
            act.wait_ge(loaded_kv, 32)
            nc.scalar.activation(m.wk_hi[:, :], raw_kv[:, 0:INNER], ACT.Copy).then_inc(cross_hi, 1)
            nc.scalar.activation(m.wv_hi[:, :], raw_kv[:, INNER:2 * INNER], ACT.Copy).then_inc(cross_hi, 1)
            for r in range(2):
                nc.scalar.activation(m.wq_hi[:, :, r, :], raw_q[:, :].rearrange("p (h c) -> p h c", h=XH),
                                     ACT.Copy).then_inc(cross_hi, 1)

            def emit(w):
                for kind, rel, i in w.steps:
                    b, par = w.batch + rel, (w.parity + rel) % 2
                    s = w.slot.get((kind, rel, i))
                    if kind == "T":
                        act.wait_ge(full["T"], b * T + i + 1)
                        nc.scalar.activation(xt_hi[:, par, i * P:(i + 1) * P], slot(s, P), ACT.Copy).then_inc(xh_done, 1)
                    if kind == "KQ":
                        act.wait_ge(full["KQ"], b * SG + i + 1)
                        wait(act, kq_ready, 2 * (b * SG + i))
                        nc.scalar.activation(round_kq[:, :, :], ps[:, 2 * s:2 * s + 2, 0:S], ACT.Copy).then_inc(round_done, 1)
                    if kind == "V":
                        act.wait_ge(full["V"], b + 1)
                        wait(act, pv_done, (b - 1) * SG)
                        nc.scalar.activation(vals[:, par, :, :, :].rearrange("p t h c -> p (t h c)"), slot(s),
                                             ACT.Copy).then_inc(v_ready, 1)
                    if kind == "EXP":
                        n = b * SH + i
                        g = i // HG
                        wait(act, pt_dve if i % 2 else pt_act, b * (SH // 2) + (i - 4 - i % 2) // 2 + 1)
                        wait(act, rsum_ready, b * SG + g - 1)
                        for j, (lo, hi) in enumerate(((0, P), (P, PV_COLS))):
                            act.wait_ge(masked_ready, T * n + j + 1)
                            nc.scalar.activation(probs[:, i % 4, lo:hi], masked[:, i % 2, lo:hi], ACT.Exp,
                                                 scale=-1.0, bias=low[:, i % 2, j:j + 1],
                                                 accum_out=sums[:, g % 2, j, i % HG:i % HG + 1]).then_inc(exp_done, 1)
                    if kind == "PT" and i % 2 == 0:
                        act.wait_ge(full["PT"], b * SH + i + 1)
                        wait(act, pv_done, b * SG + i // HG - 1)
                        nc.scalar.activation(probs_t[:, i % RING, :], slot(s, PV_COLS), ACT.Copy).then_inc(pt_act, 1)
                    if kind == "R":
                        act.wait_ge(full["R"], b * SG + i + 1)
                        wait(act, heads_ready, b * SG + i - 1)
                        nc.scalar.activation(rsum_t[:, i % 2, :], slot(s, S), ACT.Copy).then_inc(rsum_t_ready, 1)
            run_windows(act, plan, B, emit)

        @block.vector
        def _(dve):
            count = [0]

            def link(instruction):
                count[0] += 1
                instruction.then_inc(setup, 1)
                dve.wait_ge(setup, count[0])

            for t_ in (av_hi, av_lo):
                dve.memset(t_[:, :, :].bitcast(F32), 0.0)
            dve.memset(wo_pad[:, :, :], 0.0)
            link(dve.memset(part[:, :], 0.0))
            for rows, col in ((slice(32, 64), 0), (slice(96, 128), 0), (slice(64, 96), 1), (slice(96, 128), 1)):
                last = dve.memset(part[rows, col:col + 1], -1.0)
            link(last)
            dve.wait_ge(consts, 5)
            link(dve.tensor_reduce(head_of[:, :], ident[:, :].rearrange("p (q j c) -> p j q c", q=4, j=HG),
                                   AX.XY, ALU.add))
            dve.wait_ge(loaded_w, 64)
            link(dve.tensor_copy(wo_pad[:, :, 0:SD], raw[:, 3, :].rearrange("p (h c) -> p h c", h=SH)))
            dve.wait_ge(wt_full, 1)
            dve.tensor_scalar(wt[:, 0, :], slot(0, P), -SCALE, None, ALU.mult)
            link(dve.tensor_copy(wt[:, 1:3, :].rearrange("p a b -> p (a b)"), slot(0, 2 * P, P)))
            link(dve.tensor_copy(wt_hi[:, :, :], wt[:, :, :]))
            link(dve.tensor_tensor(wt_lo[:, :, :], wt[:, :, :], wt_hi[:, :, :].bitcast(F32), ALU.subtract))
            for hi, lo, n in ((aq_hi, aq_lo, 0), (ak_hi, ak_lo, 1)):
                for g in range(SG):
                    for dst, src in ((hi, wt_hi[:, n, :].bitcast(F32)), (lo, wt_lo[:, n, :])):
                        dve.tensor_copy(dst[:, g, :, :],
                                        src[:, 32 * g:32 * g + 32].unsqueeze(1).broadcast_to([P, 4, 32]))
            dve.tensor_copy(av_hi[:, :, 0:SD], wt_hi[:, 2, :].bitcast(F32).rearrange("p (h c) -> p h c", h=SH))
            dve.tensor_copy(av_lo[:, :, 0:SD], wt_lo[:, 2, :].rearrange("p (h c) -> p h c", h=SH))
            dve.wait_ge(wt_full, 2)
            dve.tensor_copy(wo_t[:, :, :].rearrange("p g d -> p (g d)"), slot(1, SG * D)).then_inc(weights, 1)
            dve.wait_ge(loaded_b, 16)

            def emit(w):
                for kind, rel, i in w.steps:
                    b, par = w.batch + rel, (w.parity + rel) % 2
                    s = w.slot.get((kind, rel, i))
                    if kind == "T":
                        dve.wait_ge(xh_done, b * T + i + 1)
                        dve.tensor_tensor(xt_lo[:, par, i * P:(i + 1) * P], slot(s, P),
                                          xt_hi[:, par, i * P:(i + 1) * P].bitcast(F32), ALU.subtract).then_inc(x_ready, 1)
                    if kind == "KQ":
                        dve.wait_ge(round_done, b * SG + i + 1)
                        dve.scalar_tensor_tensor(out=k_parts[:, i, :], in0=round_kq[:, 0, :].bitcast(F32),
                                                 scalar=part[:, 0:1], in1=ps[:, 2 * s, 0:S],
                                                 op0=ALU.mult, op1=ALU.add).then_inc(kq_ready, 1)
                        dve.scalar_tensor_tensor(out=q_parts[:, i % 2, :], in0=round_kq[:, 1, :].bitcast(F32),
                                                 scalar=part[:, 1:2], in1=ps[:, 2 * s + 1, 0:S],
                                                 op0=ALU.mult, op1=ALU.add).then_inc(kq_ready, 1)
                    if kind == "QH":
                        g = i // HG
                        dve.wait_ge(kq_ready, 2 * (b * SG + g) + 2)
                        wait(dve, full["S"], b * SH + i - 3)
                        dve.tensor_scalar(q_head[:, i % 4, :], q_parts[:, g % 2, :].bitcast(F32),
                                          head_of[:, i % HG:i % HG + 1], None, ALU.mult).then_inc(qh_ready, 1)
                    if kind == "S":
                        n = b * SH + i
                        dve.wait_ge(consts, 5)
                        dve.wait_ge(full["S"], n + 1)
                        wait(dve, exp_done, T * (n - 1))
                        hold(dve, spare[:, i % 2:i % 2 + 1])
                        for j, (lo, hi) in enumerate(((0, P), (P, PV_COLS))):
                            dve.tensor_tensor_reduce(masked[:, i % 2, lo:hi], slot(s, hi - lo, j * S),
                                                     causal[:, S - (hi - lo):S], 1.0, 3e38, ALU.add, ALU.min,
                                                     low[:, i % 2, j:j + 1]).then_inc(masked_ready, 1)
                    if kind == "PT" and i % 2 == 1:
                        dve.wait_ge(full["PT"], b * SH + i + 1)
                        wait(dve, pv_done, b * SG + i // HG - 1)
                        dve.tensor_copy(probs_t[:, i % RING, :], slot(s, PV_COLS)).then_inc(pt_dve, 1)
                    if kind == "R":
                        n = b * SG + i
                        dve.wait_ge(exp_done, T * HG * (n + 1))
                        wait(dve, wide_ready, n - 1)
                        dve.reciprocal(rsum[:, i % 2, :, :], sums[:, i % 2, :, :]).then_inc(rsum_ready, 1)
                    if kind == "NORM":
                        n = b * SG + i
                        dve.wait_ge(rsum_t_ready, n + 1)
                        dve.wait_ge(pv_done, n + 1)
                        wait(dve, full["OUT"], b * T)
                        dve.tensor_tensor(heads_t[:, i, :], ps[:, O_BANK + i % 2, 0:S], rsum_t[:, i % 2, :],
                                          ALU.mult).then_inc(heads_ready, 1)
                    if kind == "OUT":
                        dve.wait_ge(full["OUT"], b * T + i + 1)
                        dve.tensor_tensor(state[:, bass.ds(b * T + i, 1), :], slot(s, D).unsqueeze(1),
                                          x_in[:, par, i:i + 1, :], ALU.add).then_inc(added, 1)
                        if i == 0:
                            for j in range(CT):
                                last = dve.bn_stats(stats[:, bass.ds(b * KT + j, 1), :], ctx_all[:, bass.ds(b * CT + j, 1), :])
                        else:
                            dve.wait_ge(added, b * T + T)
                            for j in range(T):
                                last = dve.bn_stats(stats[:, bass.ds(b * KT + CT + j, 1), :], state[:, bass.ds(b * T + j, 1), :])
                            last.then_inc(measured, 1)
            run_windows(dve, plan, B, emit)

        @block.tensor
        def _(pe):
            pe.wait_ge(consts, 4)
            pe.wait_ge(loaded_w, 64)
            for i in range(3):
                last = nc.tensor.transpose(slot(0, P, i * P), raw[:, i, :], ident[:, :])
            last.then_inc(wt_full, 1)
            pe.wait_ge(setup, 4)
            for g in range(SG):
                last = nc.tensor.transpose(slot(1, P, g * P),
                                           wo_pad[:, 4 * g:4 * g + 4, :].rearrange("p h c -> p (h c)"), ident[:, :])
            last.then_inc(wt_full, 1)
            pe.wait_ge(weights, 1)

            def emit(w):
                for kind, rel, i in w.steps:
                    b, par = w.batch + rel, (w.parity + rel) % 2
                    s = w.slot.get((kind, rel, i))
                    if s is not None and w.before[kind, rel, i]:
                        k0, r0, i0 = w.before[kind, rel, i]
                        wait(pe, *taken(k0, w.batch + r0, i0))
                    if kind == "T":
                        if i == 0:
                            pe.wait_ge(loaded_x, 16 * (b + 1))
                        nc.tensor.transpose(slot(s, P), x_in[:, par, i, :], ident[:, :]).then_inc(full["T"], 1)
                    if kind == "KQ":
                        pe.wait_ge(x_ready, T * (b + 1))
                        for bank, hi, lo in ((0, ak_hi, ak_lo), (1, aq_hi, aq_lo)):
                            o = slot(s, S, bank * BANK)
                            wh, wl = (a[:, i, :, :].rearrange("p r c -> p (r c)") for a in (hi, lo))
                            nc.tensor.matmul(o, wh, xt_hi[:, par, :], start=True, stop=False)
                            nc.tensor.matmul(o, wh, xt_lo[:, par, :], start=False, stop=False)
                            last = nc.tensor.matmul(o, wl, xt_hi[:, par, :], start=False, stop=True)
                        last.then_inc(full["KQ"], 1)
                    if kind == "V":
                        pe.wait_ge(x_ready, T * (b + 1))
                        wh, wl = (a[:, :, :].rearrange("p h c -> p (h c)") for a in (av_hi, av_lo))
                        for j in range(T):
                            o = slot(s, BANK, j * BANK)
                            xh, xl = (a[:, par, j * P:(j + 1) * P] for a in (xt_hi, xt_lo))
                            nc.tensor.matmul(o, xh, wh, start=True, stop=False)
                            nc.tensor.matmul(o, xh, wl, start=False, stop=False)
                            last = nc.tensor.matmul(o, xl, wh, start=False, stop=True)
                        last.then_inc(full["V"], 1)
                    if kind == "S":
                        pe.wait_ge(qh_ready, b * SH + i + 1)
                        for j in range(T):
                            last = nc.tensor.matmul(slot(s, S, j * S), q_head[:, i % 4, j * P:(j + 1) * P],
                                                    k_parts[:, i // HG, :], start=True, stop=True)
                        last.then_inc(full["S"], 1)
                    if kind == "PT":
                        pe.wait_ge(exp_done, T * (b * SH + i + 1))
                        for j in range(3):
                            last = nc.tensor.transpose(slot(s, P, j * P), probs[:, i % 4, j * P:(j + 1) * P], ident[:, :])
                        last.then_inc(full["PT"], 1)
                    if kind == "PV":
                        n = b * SG + i
                        pe.wait_ge(pt_act, (n + 1) * HG // 2)
                        pe.wait_ge(pt_dve, (n + 1) * HG // 2)
                        pe.wait_ge(v_ready, b + 1)
                        wait(pe, heads_ready, n - 1)
                        for kt, lo in ((0, 0), (1, P)):
                            for j in range(HG):
                                h = i * HG + j
                                last = nc.tensor.matmul(ps[32 * j:32 * j + 32, O_BANK + i % 2, lo:S],
                                                        vals[:, par, kt, h, :],
                                                        probs_t[:, h % RING, kt * S:kt * S + S - lo],
                                                        start=(kt == 0), stop=(kt == 1), skip_group_check=True)
                        last.then_inc(pv_done, 1)
                    if kind == "R":
                        pe.wait_ge(wide_ready, b * SG + i + 1)
                        for j in range(T):
                            last = nc.tensor.transpose(slot(s, P, j * P),
                                                       rsum_wide[:, i % 2, j, :, :].rearrange("p h c -> p (h c)"), ident[:, :])
                        last.then_inc(full["R"], 1)
                    if kind == "OUT":
                        pe.wait_ge(heads_ready, SG * (b + 1))
                        for g in range(SG):
                            last = nc.tensor.matmul(slot(s, D), heads_t[:, g, i * P:(i + 1) * P], wo_t[:, g, :],
                                                    start=(g == 0), stop=(g == SG - 1))
                        last.then_inc(full["OUT"], 1)
            run_windows(pe, plan, B, emit)
    mem.close()


def cross_attention(nc, sem, sb, ps, slot, m):
    B, S, D, T, C, CT, KT, KEYS = m.B, m.S, m.D, m.T, m.C, m.CT, m.KT, m.KEYS
    XH, XD, PAIRS, INNER = m.XH, m.XD, m.PAIRS, m.INNER
    ident, state, stats, mean, rstd, gb = m.ident, m.state, m.stats, m.mean, m.rstd, m.gb
    UNITS = XH * T
    Q_SCALE = -float(XD) ** -0.5

    mem = ExitStack()
    bar = sb(mem, "bar", [P, 2, KEYS])
    normed = sb(mem, "normed", [P, KT, D])
    y = sb(mem, "y", [P, KEYS])
    y_hi = sb(mem, "y_hi", [P, 2, KEYS], F32R)
    y_lo = sb(mem, "y_lo", [P, 2, KEYS], F32R)
    vals = sb(mem, "xvals", [P, 2, KT, INNER])
    k_parts = sb(mem, "xk_parts", [P, 2, 2, KEYS], F32R)
    q_hi = sb(mem, "q_hi", [P, 2, 2, S], F32R)
    q_lo = sb(mem, "q_lo", [P, 2, 2, S], F32R)
    masked = sb(mem, "xmasked", [P, 2, KEYS])
    spare = sb(mem, "xspare", [P, 2])
    low = sb(mem, "xlow", [P, 2])
    probs = sb(mem, "xprobs", [P, 4, KEYS])
    sums = sb(mem, "xsums", [P, 4, 2, T])
    rsum = sb(mem, "xrsum", [P, 2, 2, T])
    rsum_wide = sb(mem, "xrsum_wide", [P, 2, T, 2, XD])
    rsum_t = sb(mem, "xrsum_t", [P, 2, S])
    probs_t = sb(mem, "xprobs_t", [P, 2, KT, T, P])
    heads_t = sb(mem, "xheads_t", [P, PAIRS, S])

    bar_zeroed = sem("x_bar_zeroed")
    bar_ready = sem("x_bar_ready")
    normed_ready = sem("x_normed_ready")
    full = {k: sem(f"x_{k}_full") for k in ("T", "K", "Q", "V", "S", "PT", "R", "OUT")}
    y_ready = sem("x_y_ready")
    yh_done, y_split = sem("x_yh_done"), sem("x_y_split")
    kh_done, k_ready = sem("x_kh_done"), sem("x_k_ready")
    qh_done, q_ready = sem("x_qh_done"), sem("x_q_ready")
    v_ready = sem("x_v_ready")
    masked_ready = sem("x_masked_ready")
    exp_done = sem("x_exp_done")
    pt_act, pt_dve = sem("x_pt_act"), sem("x_pt_dve")
    rsum_ready = sem("x_rsum_ready")
    wide_ready = sem("x_wide_ready")
    rsum_t_ready = sem("x_rsum_t_ready")
    pv_done = sem("x_pv_done")
    heads_ready = sem("x_heads_ready")
    added = sem("x_added")
    measured = sem("x_measured")

    jobs = {"T", "K", "Q", "V", "S", "PT", "R", "OUT"}

    def taken(kind, batch, i):
        if kind == "PT":
            return (pt_dve if i % 2 else pt_act), batch * (UNITS // 2) + i // 2 + 1
        semaphore, per, extra = {
            "T": (y_ready, 2, 2), "K": (k_ready, 2 * PAIRS, 2), "Q": (q_ready, PAIRS, 1), "V": (v_ready, KT, 1),
            "S": (masked_ready, UNITS, 1), "R": (rsum_t_ready, PAIRS, 1), "OUT": (added, 1, 1)}[kind]
        return semaphore, batch * per + i * extra + extra

    steps = []
    for t in range(UNITS):
        steps.append(("S", 0, t))
        steps.append(("PT", (t - 3) // UNITS, (t - 3) % UNITS))
        steps.append(("EXP", 0, t))
        if t % 2 == 0:
            head = (t - 6) // 2
            steps.append(("PV", head // XH, head % XH))
        if t % 4 == 1:
            pair = (t - 9) // 4
            steps.append(("NORM", pair // PAIRS, pair % PAIRS))
            pair = t // 4 + 1
            steps.append(("K", pair // PAIRS, pair % PAIRS))
        if t % 4 == 2:
            pair = (t - 6) // 4
            steps.append(("R", pair // PAIRS, pair % PAIRS))
        if t % 4 == 3:
            pair = t // 4 + 1
            steps.append(("Q", pair // PAIRS, pair % PAIRS))
        if t == 7:
            steps.append(("OUT", -1, 0))
        if t == 8:
            steps += [("NORMED", 1, 0), ("BAR", 1, 0)]
        if t == 11:
            steps.append(("T", 1, 0))
        if t >= 15 and t % 2 == 1 and (t - 15) // 2 < KT:
            steps.append(("V", 1, (t - 15) // 2))
    plan = plan_windows(B, steps, jobs, 2)

    with nc.Block() as block:

        @block.gpsimd
        def _(pool):
            def emit(w):
                for kind, rel, i in w.steps:
                    b, par = w.batch + rel, (w.parity + rel) % 2
                    if kind == "T":
                        pool.wait_ge(yh_done, b + 1)
                        pool.tensor_tensor(y_lo[:, par, :], y[:, :], y_hi[:, par, :].bitcast(F32),
                                           ALU.subtract).then_inc(y_split, 1)
                    if kind == "R":
                        pool.wait_ge(rsum_ready, b * PAIRS + i + 1)
                        for j in range(T):
                            last = pool.tensor_tensor(rsum_wide[:, i % 2, j, :, :],
                                                      m.ones[:, 0:P].rearrange("p (a c) -> p a c", c=XD),
                                                      rsum[:, i % 2, :, j:j + 1].broadcast_to([P, 2, XD]), ALU.mult)
                        last.then_inc(wide_ready, 1)
            run_windows(pool, plan, B, emit)

        @block.scalar
        def _(act):
            def emit(w):
                for kind, rel, i in w.steps:
                    b, par = w.batch + rel, (w.parity + rel) % 2
                    s = w.slot.get((kind, rel, i))
                    if kind == "T":
                        act.wait_ge(full["T"], b + 1)
                        wait(act, y_split, b)
                        for lo, hi, g in ((0, C, 0), (C, KEYS, 2)):
                            nc.scalar.activation(y[:, lo:hi], slot(s, hi - lo, lo), ACT.Identity,
                                                 scale=gb[:, g:g + 1], bias=gb[:, g + 1:g + 2]).then_inc(y_ready, 1)
                    if kind == "K":
                        act.wait_ge(full["K"], b * PAIRS + i + 1)
                        for h, rows in ((0, slice(0, XD)), (1, slice(XD, P))):
                            nc.scalar.activation(k_parts[rows, i % 2, h, :], slot(s, KEYS)[rows], ACT.Copy).then_inc(kh_done, 1)
                    if kind == "Q":
                        act.wait_ge(full["Q"], b * PAIRS + i + 1)
                        nc.scalar.activation(q_hi[:, i % 2, :, :].rearrange("p h t -> p (h t)"), slot(s, 2 * S),
                                             ACT.Copy, scale=Q_SCALE).then_inc(qh_done, 1)
                    if kind == "V":
                        act.wait_ge(full["V"], b * KT + i + 1)
                        wait(act, pv_done, (b - 1) * XH)
                        nc.scalar.activation(vals[:, par, i, :], slot(s), ACT.Copy).then_inc(v_ready, 1)
                    if kind == "EXP":
                        pair, n = i // 4, b * UNITS + i
                        if i % 2:
                            wait(act, pt_dve, b * (UNITS // 2) + (i - 5) // 2 + 1)
                        act.wait_ge(masked_ready, n + 1)
                        nc.scalar.activation(probs[:, i % 4, :], masked[:, i % 2, :], ACT.Exp, scale=-1.0,
                                             bias=low[:, i % 2:i % 2 + 1],
                                             accum_out=sums[:, pair % 4, i // 2 % 2, i % 2:i % 2 + 1]).then_inc(exp_done, 1)
                    if kind == "PT" and i % 2 == 0:
                        act.wait_ge(full["PT"], b * UNITS + i + 1)
                        wait(act, pv_done, b * XH + i // 2 - 1)
                        nc.scalar.activation(probs_t[:, i // 2 % 2, :, 0, :],
                                             slot(s, KEYS).rearrange("p (k t) -> p k t", k=KT), ACT.Copy).then_inc(pt_act, 1)
                    if kind == "R":
                        act.wait_ge(full["R"], b * PAIRS + i + 1)
                        wait(act, heads_ready, b * PAIRS + i - 1)
                        nc.scalar.activation(rsum_t[:, i % 2, :], slot(s, S), ACT.Copy).then_inc(rsum_t_ready, 1)
            run_windows(act, plan, B, emit)

        @block.vector
        def _(dve):
            dve.memset(bar[:, :, C:KEYS], 0.0).then_inc(bar_zeroed, 1)

            def emit(w):
                for kind, rel, i in w.steps:
                    b, par = w.batch + rel, (w.parity + rel) % 2
                    s = w.slot.get((kind, rel, i))
                    if kind == "NORMED":
                        for j in range(KT):
                            src = (m.ctx_all[:, bass.ds(b * CT + j, 1), :] if j < CT
                                   else state[:, bass.ds(b * T + j - CT, 1), :])
                            last = dve.tensor_scalar(normed[:, j:j + 1, :], src, mean[:, bass.ds(b * KT + j, 1)],
                                                     rstd[:, bass.ds(b * KT + j, 1)], ALU.subtract, ALU.mult)
                        last.then_inc(normed_ready, 1)
                    if kind == "BAR":
                        wait(dve, masked_ready, (b - 1) * UNITS)
                        dve.tensor_scalar(bar[:, par:par + 1, 0:C], m.keep_all[:, bass.ds(b, 1), :].bitcast(U8), -BIG, BIG,
                                          ALU.mult, ALU.add).then_inc(bar_ready, 1)
                    if kind == "T":
                        dve.wait_ge(y_ready, 2 * (b + 1))
                        dve.tensor_copy(y_hi[:, par, :], y[:, :]).then_inc(yh_done, 1)
                    if kind == "K":
                        n = b * PAIRS + i
                        for h, src, dst in ((0, slice(0, XD), slice(XD, P)), (1, slice(XD, P), slice(0, XD))):
                            dve.wait_ge(kh_done, 2 * n + h + 1)
                            if h == 0:
                                dve.wait_ge(kh_done, 2 * n + 2)
                            dve.tensor_tensor(k_parts[dst, i % 2, h, :], slot(s, KEYS)[src],
                                              k_parts[src, i % 2, h, :].bitcast(F32), ALU.subtract).then_inc(k_ready, 1)
                    if kind == "Q":
                        dve.wait_ge(qh_done, b * PAIRS + i + 1)
                        dve.scalar_tensor_tensor(out=q_lo[:, i % 2, :, :].rearrange("p h t -> p (h t)"),
                                                 in0=slot(s, 2 * S), scalar=Q_SCALE,
                                                 in1=q_hi[:, i % 2, :, :].rearrange("p h t -> p (h t)").bitcast(F32),
                                                 op0=ALU.mult, op1=ALU.subtract).then_inc(q_ready, 1)
                    if kind == "S":
                        n = b * UNITS + i
                        dve.wait_ge(bar_zeroed, 1)
                        if i == 0:
                            dve.wait_ge(bar_ready, b + 1)
                        dve.wait_ge(full["S"], n + 1)
                        wait(dve, exp_done, n - 1)
                        hold(dve, spare[:, i % 2:i % 2 + 1])
                        dve.tensor_tensor_reduce(masked[:, i % 2, :], slot(s, KEYS), bar[:, par, :], 1.0, 3e38,
                                                 ALU.add, ALU.min, low[:, i % 2:i % 2 + 1]).then_inc(masked_ready, 1)
                    if kind == "PT" and i % 2 == 1:
                        dve.wait_ge(full["PT"], b * UNITS + i + 1)
                        wait(dve, pv_done, b * XH + i // 2 - 1)
                        dve.tensor_copy(probs_t[:, i // 2 % 2, :, 1, :],
                                        slot(s, KEYS).rearrange("p (k t) -> p k t", k=KT)).then_inc(pt_dve, 1)
                    if kind == "R":
                        n = b * PAIRS + i
                        dve.wait_ge(exp_done, 4 * (n + 1))
                        wait(dve, wide_ready, n - 1)
                        dve.reciprocal(rsum[:, i % 2, :, :], sums[:, i % 4, :, :]).then_inc(rsum_ready, 1)
                    if kind == "NORM":
                        n = b * PAIRS + i
                        dve.wait_ge(rsum_t_ready, n + 1)
                        dve.wait_ge(pv_done, 2 * (n + 1))
                        wait(dve, full["OUT"], b)
                        dve.tensor_tensor(heads_t[:, i, :], ps[:, O_BANK + i % 2, 0:S], rsum_t[:, i % 2, :],
                                          ALU.mult).then_inc(heads_ready, 1)
                    if kind == "OUT":
                        dve.wait_ge(full["OUT"], b + 1)
                        tokens = state[:, bass.ds(b * T, T), :]
                        dve.tensor_tensor(tokens, slot(s, T * D).rearrange("p (t d) -> p t d", t=T), tokens,
                                          ALU.add).then_inc(added, 1)
                        dve.wait_ge(added, b + 1)
                        for j in range(T):
                            last = dve.bn_stats(stats[:, bass.ds(b * KT + CT + j, 1), :], state[:, bass.ds(b * T + j, 1), :])
                        last.then_inc(measured, 1)
            run_windows(dve, plan, B, emit)

        @block.tensor
        def _(pe):
            wk_hi, wk_lo, wv_hi, wv_lo = m.wk_hi, m.wk_lo, m.wv_hi, m.wv_lo

            def emit(w):
                for kind, rel, i in w.steps:
                    b, par = w.batch + rel, (w.parity + rel) % 2
                    s = w.slot.get((kind, rel, i))
                    if s is not None and w.before[kind, rel, i]:
                        k0, r0, i0 = w.before[kind, rel, i]
                        wait(pe, *taken(k0, w.batch + r0, i0))
                    if kind == "T":
                        pe.wait_ge(normed_ready, b + 1)
                        for j in range(KT):
                            last = nc.tensor.transpose(slot(s, P, j * P), normed[:, j, :], ident[:, :])
                        last.then_inc(full["T"], 1)
                    if kind == "K":
                        pe.wait_ge(y_split, b + 1)
                        wh, wl = (a[:, i * P:(i + 1) * P] for a in (wk_hi, wk_lo))
                        for lo, hi in ((0, C), (C, KEYS)):
                            o = slot(s, hi - lo, lo)
                            nc.tensor.matmul(o, wh, y_hi[:, par, lo:hi], start=True, stop=False)
                            nc.tensor.matmul(o, wh, y_lo[:, par, lo:hi], start=False, stop=False)
                            last = nc.tensor.matmul(o, wl, y_hi[:, par, lo:hi], start=False, stop=True)
                        last.then_inc(full["K"], 1)
                    if kind == "Q":
                        pe.wait_ge(y_split, b + 1)
                        for h in range(2):
                            o = slot(s, S, h * S)
                            wh, wl = (a[:, 2 * i + h, :, :].rearrange("p r c -> p (r c)") for a in (m.wq_hi, m.wq_lo))
                            nc.tensor.matmul(o, wh, y_hi[:, par, C:KEYS], start=True, stop=False)
                            nc.tensor.matmul(o, wh, y_lo[:, par, C:KEYS], start=False, stop=False)
                            last = nc.tensor.matmul(o, wl, y_hi[:, par, C:KEYS], start=False, stop=True)
                        last.then_inc(full["Q"], 1)
                    if kind == "V":
                        pe.wait_ge(y_split, b + 1)
                        yh, yl = (a[:, par, i * P:(i + 1) * P] for a in (y_hi, y_lo))
                        for c in range(INNER // BANK):
                            o, cols = slot(s, BANK, c * BANK), slice(c * BANK, (c + 1) * BANK)
                            nc.tensor.matmul(o, yh, wv_hi[:, cols], start=True, stop=False)
                            nc.tensor.matmul(o, yh, wv_lo[:, cols], start=False, stop=False)
                            last = nc.tensor.matmul(o, yl, wv_hi[:, cols], start=False, stop=True)
                        last.then_inc(full["V"], 1)
                    if kind == "S":
                        pair, h, t = i // 4, i // 2 % 2, i % 2
                        if i % 4 == 0:
                            pe.wait_ge(k_ready, 2 * (b * PAIRS + pair + 1))
                            pe.wait_ge(q_ready, b * PAIRS + pair + 1)
                        for lo, hi in ((0, C), (C, KEYS)):
                            for q, first in ((q_hi, True), (q_lo, False)):
                                last = nc.tensor.matmul(slot(s, hi - lo, lo), q[:, pair % 2, h, t * P:(t + 1) * P],
                                                        k_parts[:, pair % 2, h, lo:hi], start=first, stop=not first)
                        last.then_inc(full["S"], 1)
                    if kind == "PT":
                        pe.wait_ge(exp_done, b * UNITS + i + 1)
                        for j in range(KT):
                            last = nc.tensor.transpose(slot(s, P, j * P), probs[:, i % 4, j * P:(j + 1) * P], ident[:, :])
                        last.then_inc(full["PT"], 1)
                    if kind == "PV":
                        n = b * XH + i
                        pe.wait_ge(pt_act, n + 1)
                        pe.wait_ge(pt_dve, n + 1)
                        if i == 0:
                            pe.wait_ge(v_ready, KT * (b + 1))
                        if i % 2 == 0:
                            wait(pe, heads_ready, b * PAIRS + i // 2 - 1)
                        rows = slice((i % 2) * XD, (i % 2) * XD + XD)
                        for j in range(KT):
                            last = nc.tensor.matmul(ps[rows, O_BANK + i // 2 % 2, 0:S], vals[:, par, j, i * XD:(i + 1) * XD],
                                                    probs_t[:, i % 2, j, :, :].rearrange("p t q -> p (t q)"),
                                                    start=(j == 0), stop=(j == KT - 1), skip_group_check=True)
                        last.then_inc(pv_done, 1)
                    if kind == "R":
                        pe.wait_ge(wide_ready, b * PAIRS + i + 1)
                        for j in range(T):
                            last = nc.tensor.transpose(slot(s, P, j * P),
                                                       rsum_wide[:, i % 2, j, :, :].rearrange("p h c -> p (h c)"), ident[:, :])
                        last.then_inc(full["R"], 1)
                    if kind == "OUT":
                        pe.wait_ge(heads_ready, PAIRS * (b + 1))
                        for t in range(T):
                            for pair in range(PAIRS):
                                last = nc.tensor.matmul(slot(s, D, t * D), heads_t[:, pair, t * P:(t + 1) * P],
                                                        m.wout[:, pair, :], start=(pair == 0), stop=(pair == PAIRS - 1))
                        last.then_inc(full["OUT"], 1)
            run_windows(pe, plan, B, emit)
    mem.close()


def experts(nc, sem, sb, ps, slot, m):
    B, S, D, T, CT, KT, E, NE, HID, HB = m.B, m.S, m.D, m.T, m.CT, m.KT, m.E, m.NE, m.HID, m.HB
    ident, state, stats, w_rt = m.ident, m.state, m.stats, m.w_rt
    TILES = B * T

    mem = ExitStack()
    w_up = sb(mem, "w_up", [P, 2, NE, HID])
    up_hi = sb(mem, "up_hi", [P, 2, NE, HID], F32R)
    up_lo = sb(mem, "up_lo", [P, 2, NE, HID], F32R)
    w_down = sb(mem, "w_down", [P, NE, HB, D])
    xt = sb(mem, "xt", [P, TILES * P])
    xt_hi = sb(mem, "cxt_hi", [P, TILES * P], F32R)
    xt_lo = sb(mem, "cxt_lo", [P, TILES * P], F32R)
    logits = sb(mem, "logits", [P, TILES, E])
    index = sb(mem, "index", [P, TILES, E])
    best = sb(mem, "best", [P, 2, TILES])
    first = sb(mem, "first", [P, TILES])
    chosen = sb(mem, "chosen", [P, 2, TILES, E])
    scratch = sb(mem, "scratch", [P, TILES, E])
    gap = sb(mem, "gap", [P, TILES])
    gate = sb(mem, "gate", [P, 2, TILES])
    gates = sb(mem, "gates", [P, TILES, E])
    silu = sb(mem, "silu", [P, 3, HB * S])
    hidden = sb(mem, "hidden", [P, 3, HB * S])

    loaded = [sem(f"e_loaded{n}") for n in range(2)]
    loaded_down = sem("e_loaded_down")
    index_ready = sem("e_index_ready")
    up_hi_done, up_ready = sem("e_up_hi_done"), sem("e_up_ready")
    xt_full, xt_copied = sem("e_xt_full"), sem("e_xt_copied")
    xh_done, x_ready = sem("e_xh_done"), sem("e_x_ready")
    logits_full = sem("e_logits_full")
    chain = sem("e_chain")
    gap_ready, exp_gap = sem("e_gap_ready"), sem("e_exp_gap")
    gates_ready = sem("e_gates_ready")
    full = {k: sem(f"e_{k}_full") for k in ("H", "Y")}
    silu_done = sem("e_silu_done")
    hidden_ready = sem("e_hidden_ready")
    summed = sem("e_summed")
    measured = sem("e_measured")

    jobs = {"H", "Y"}

    def taken(kind, batch, i):
        if kind == "H":
            return hidden_ready, batch * NE + i + 1
        return summed, (batch * NE + i + 1) * T

    LAG = 2
    steps = []
    for t in range(NE):
        steps.append(("H", 0, t))
        steps.append(("Y", (t - LAG) // NE, (t - LAG) % NE))
    plan = plan_windows(B, steps, jobs, 1)

    with nc.Block() as block:

        @block.sync
        def _(sp):
            for n, (shared, routed) in enumerate(((m.sw1, m.w1), (m.sw3, m.w3))):
                sp.dma_start(w_up[:, n, 0, :], shared).then_inc(loaded[n], 16)
                sp.dma_start(w_up[:, n, 1:NE, :], routed.rearrange("e d h -> d e h")).then_inc(loaded[n], 16)
            sp.dma_start(w_down[:, 0, :, :], m.sw2.rearrange("(k p) d -> p k d", p=P)).then_inc(loaded_down, 16)
            sp.dma_start(w_down[:, 1:NE, :, :].rearrange("p e k d -> p (e k) d"),
                         m.w2.rearrange("e (k p) d -> p (e k) d", p=P)).then_inc(loaded_down, 16)

        @block.gpsimd
        def _(pool):
            for e in range(E):
                last = pool.memset(index[:, :, e:e + 1], float(e - E))
            last.then_inc(index_ready, 1)
            pool.wait_ge(up_hi_done, 2)
            pool.tensor_tensor(up_lo[:, 1, :, :], w_up[:, 1, :, :], up_hi[:, 1, :, :].bitcast(F32),
                               ALU.subtract).then_inc(up_ready, 1)

        @block.scalar
        def _(act):
            for n in range(2):
                act.wait_ge(loaded[n], 32)
                nc.scalar.activation(up_hi[:, n, :, :], w_up[:, n, :, :], ACT.Copy).then_inc(up_hi_done, 1)
            for n in range(TILES // 8):
                act.wait_ge(xt_full, n + 1)
                nc.scalar.activation(xt[:, n * 8 * P:(n + 1) * 8 * P], slot(n), ACT.Copy).then_inc(xt_copied, 1)
            act.wait_ge(gap_ready, 1)
            nc.scalar.activation(gap[:, :], gap[:, :], ACT.Exp).then_inc(exp_gap, 1)

            def emit(w):
                for kind, rel, i in w.steps:
                    if kind == "H":
                        n, s = (w.batch + rel) * NE + i, w.slot[kind, rel, i]
                        act.wait_ge(full["H"], n + 1)
                        wait(act, hidden_ready, n - 2)
                        nc.scalar.activation(silu[:, i % 3, :],
                                             slot(s, HB * S), ACT.Silu).then_inc(silu_done, 1)
            run_windows(act, plan, B, emit)

        @block.vector
        def _(dve):
            count = [0]

            def link(instruction):
                count[0] += 1
                instruction.then_inc(chain, 1)
                dve.wait_ge(chain, count[0])

            for n in range(TILES // 8):
                cols = slice(n * 8 * P, (n + 1) * 8 * P)
                dve.wait_ge(xt_copied, n + 1)
                dve.tensor_copy(xt_hi[:, cols], xt[:, cols]).then_inc(xh_done, 1)
                dve.wait_ge(xh_done, n + 1)
                dve.tensor_tensor(xt_lo[:, cols], xt[:, cols], xt_hi[:, cols].bitcast(F32), ALU.subtract).then_inc(x_ready, 1)
            dve.wait_ge(up_hi_done, 1)
            dve.tensor_tensor(up_lo[:, 0, :, :], w_up[:, 0, :, :], up_hi[:, 0, :, :].bitcast(F32),
                              ALU.subtract).then_inc(up_ready, 1)
            dve.wait_ge(logits_full, 1)
            link(dve.tensor_copy(logits[:, :, :], slot(2, TILES * E).rearrange("p (t e) -> p t e", e=E)))
            dve.wait_ge(index_ready, 1)
            for n in range(2):
                top, pick = best[:, n, :], chosen[:, n, :, :]
                link(dve.tensor_reduce(top, logits[:, :, :], AX.X, ALU.max))
                link(dve.tensor_tensor(scratch[:, :, :], logits[:, :, :], top.unsqueeze(2).broadcast_to([P, TILES, E]),
                                       ALU.is_equal))
                link(dve.tensor_tensor(scratch[:, :, :], scratch[:, :, :], index[:, :, :], ALU.mult))
                link(dve.tensor_reduce(first[:, :], scratch[:, :, :], AX.X, ALU.min))
                link(dve.tensor_tensor(pick, index[:, :, :], first[:, :].unsqueeze(2).broadcast_to([P, TILES, E]),
                                       ALU.is_equal))
                if n == 0:
                    link(dve.scalar_tensor_tensor(out=logits[:, :, :], in0=pick, scalar=-3e38, in1=logits[:, :, :],
                                                  op0=ALU.mult, op1=ALU.add))
            dve.tensor_tensor(gap[:, :], best[:, 1, :], best[:, 0, :], ALU.subtract).then_inc(gap_ready, 1)
            dve.wait_ge(exp_gap, 1)
            link(dve.tensor_scalar(gate[:, 0, :], gap[:, :], 1.0, None, ALU.add))
            link(dve.reciprocal(gate[:, 0, :], gate[:, 0, :]))
            link(dve.tensor_tensor(gate[:, 1, :], gate[:, 0, :], gap[:, :], ALU.mult))
            for n in range(2):
                link(dve.tensor_tensor(chosen[:, n, :, :], chosen[:, n, :, :],
                                       gate[:, n, :].unsqueeze(2).broadcast_to([P, TILES, E]), ALU.mult))
            dve.tensor_tensor(gates[:, :, :], chosen[:, 0, :, :], chosen[:, 1, :, :], ALU.add).then_inc(gates_ready, 1)
            dve.wait_ge(gates_ready, 1)

            def emit(w):
                for kind, rel, i in w.steps:
                    b, s = w.batch + rel, w.slot[kind, rel, i]
                    n = b * NE + i
                    if kind == "H":
                        dve.wait_ge(silu_done, n + 1)
                        wait(dve, full["Y"], n - 2)
                        dve.tensor_tensor(hidden[:, i % 3, :], slot(s, HB * S, BANK),
                                          silu[:, i % 3, :], ALU.mult).then_inc(hidden_ready, 1)
                    if kind == "Y":
                        dve.wait_ge(full["Y"], n + 1)
                        for j in range(T):
                            tokens = state[:, bass.ds(b * T + j, 1), :]
                            y = slot(s, D, j * D).unsqueeze(1)
                            wait(dve, summed, n * T + j - 1)
                            if i == 0:
                                dve.tensor_tensor(tokens, y, tokens, ALU.add).then_inc(summed, 1)
                            else:
                                at = gates[:, bass.ds(b * T + j, 1), i - 1:i].rearrange("p a b -> p (a b)")
                                dve.scalar_tensor_tensor(out=tokens, in0=y, scalar=at, in1=tokens,
                                                         op0=ALU.mult, op1=ALU.add).then_inc(summed, 1)
                        if i == NE - 1:
                            dve.wait_ge(summed, (n + 1) * T)
                            for j in range(T):
                                last = dve.bn_stats(stats[:, bass.ds(b * KT + CT + j, 1), :], state[:, bass.ds(b * T + j, 1), :])
                            last.then_inc(measured, 1)
            run_windows(dve, plan, B, emit)

        @block.tensor
        def _(pe):
            for n in range(TILES // 8):
                for j in range(8):
                    last = nc.tensor.transpose(slot(n, P, j * P), state[:, 8 * n + j, :], ident[:, :])
                last.then_inc(xt_full, 1)
            for i in range(TILES):
                if i % 8 == 0:
                    pe.wait_ge(xt_copied, i // 8 + 1)
                last = nc.tensor.matmul(slot(2, E, i * E), xt[:, i * P:(i + 1) * P], w_rt[:, :], start=True, stop=True)
            last.then_inc(logits_full, 1)
            pe.wait_ge(x_ready, TILES // 8)
            pe.wait_ge(up_ready, 2)
            pe.wait_ge(loaded_down, 32)
            pe.wait_ge(chain, 1)

            def emit(w):
                for kind, rel, i in w.steps:
                    b, s = w.batch + rel, w.slot[kind, rel, i]
                    n = b * NE + i
                    if w.before[kind, rel, i]:
                        k0, r0, i0 = w.before[kind, rel, i]
                        wait(pe, *taken(k0, w.batch + r0, i0))
                    if kind == "H":
                        xh, xl = (a[:, bass.ds(b * S, S)] for a in (xt_hi, xt_lo))
                        for part in range(2):
                            for k in range(HB):
                                o = slot(s, S, part * BANK + k * S)
                                wh, wl = (a[:, part, i, k * P:(k + 1) * P] for a in (up_hi, up_lo))
                                nc.tensor.matmul(o, wh, xh, start=True, stop=False)
                                nc.tensor.matmul(o, wh, xl, start=False, stop=False)
                                last = nc.tensor.matmul(o, wl, xh, start=False, stop=True)
                        last.then_inc(full["H"], 1)
                    if kind == "Y":
                        pe.wait_ge(hidden_ready, n + 1)
                        for j in range(T):
                            for k in range(HB):
                                last = nc.tensor.matmul(slot(s, D, j * D),
                                                        hidden[:, i % 3, k * S + j * P:k * S + (j + 1) * P],
                                                        w_down[:, i, k, :], start=(k == 0), stop=(k == HB - 1))
                        last.then_inc(full["Y"], 1)
            run_windows(pe, plan, B, emit)
    mem.close()


INPUTS = ["x", "ctx_1024", "mask_BxS2_bk0", "L0_attn_q_proj_weight", "L0_attn_k_proj_weight",
          "L0_attn_v_proj_weight", "L0_attn_o_proj_weight", "L0_xattn_g1", "L0_xattn_b1", "L0_xattn_g2",
          "L0_xattn_b2", "L0_xattn_Wq", "L0_xattn_Wkv", "L0_xattn_Wout", "L0_ffn_w_router", "L0_ffn_w1",
          "L0_ffn_w3", "L0_ffn_w2", "L0_ffn_sw1", "L0_ffn_sw3", "L0_ffn_sw2"]


def kernel(**inputs):
    import numpy as np
    from concourse import bacc
    from concourse.bass_utils import run_bass_kernel_spmd

    nc = bacc.Bacc("TRN2", target_bir_lowering=False, num_devices=1)
    arrays, args = {}, []
    for name in INPUTS:
        a = np.ascontiguousarray(inputs[name])
        if a.dtype == np.bool_:
            a = a.view(np.uint32)
        arrays[f"in_{name}"] = a
        args.append(nc.dram_tensor(f"in_{name}", a.shape, mybir.dt.from_np(a.dtype), kind="ExternalInput").ap())
    out = nc.dram_tensor("out", inputs["x"].shape, F32, kind="ExternalOutput").ap()
    decoder_layer(nc, *args, out)
    return run_bass_kernel_spmd(nc, [arrays], core_ids=[0]).results[0]["out"]
```

```python
from contextlib import ExitStack

import concourse.bass as bass
from concourse import mybir

ALU = mybir.AluOpType
ACT = mybir.ActivationFunctionType
AX = mybir.AxisListType
F32 = mybir.dt.float32
F32R = mybir.dt.float32r
U8 = mybir.dt.uint8
U32 = mybir.dt.uint32

P = 128
BANK = 512
SLOTS = 3
O_BANK = 2 * SLOTS
BIG = 1e30
EPS = 1e-5


class Shared:
    pass


class Order:

    def __init__(self, batches, units, starts):
        self.batches = batches
        due = []
        for kind, (count, first) in starts.items():
            for i in range(count):
                at = first + i * units / count
                due.append((at % units, kind, int(-(at // units)), i))
        due.sort(key=lambda d: d[0])
        self.steps = [d[1:] for d in due]
        assert all(-1 <= rel <= 1 for _, rel, _ in self.steps)

    def window(self, w):
        return [s for s in self.steps if 0 <= w + s[1] < self.batches]

    def run(self, engine, emit, unroll):
        def one(w, value):
            for kind, rel, i in self.window(w):
                emit(kind, value + rel, (w + rel) % 2, i)
        one(-1, -1)
        one(0, 0)
        with engine.Fori(0, (self.batches - 2) // unroll) as turn:
            for n in range(unroll):
                one(1 + n, turn * unroll + 1 + n)
        one(self.batches - 1, self.batches - 1)
        one(self.batches, self.batches)


class Turns:

    def __init__(self, order, kinds, places):
        self.batches, self.places = order.batches, places
        self.mine = [s for s in order.steps if s[0] in kinds]
        assert len(self.mine) % places == 0
        self.at = {(kind, i): n for n, (kind, _, i) in enumerate(self.mine)}

    def place(self, kind, i):
        return self.at[kind, i] % self.places

    def before(self, kind, batch, i):
        while True:
            n = self.at[kind, i]
            rel = self.mine[n][1]
            kind, rel2, i = self.mine[n - self.places]
            batch = batch + (rel2 - rel - (n < self.places))
            if not isinstance(batch, int) or 0 <= batch < self.batches:
                return kind, batch, i
            if batch < -2:
                return None


def hold(dve, place):
    dve.memset(place, 0.0)


def wait(engine, semaphore, count):
    if not isinstance(count, int) or count > 0:
        engine.wait_ge(semaphore, count)


def decoder_layer(nc, x, ctx, mask, wq, wk, wv, wo, g1, b1, g2, b2, xwq, xwkv, xwout,
                  w_router, w1, w3, w2, sw1, sw3, sw2, out):
    B, S, D = x.shape
    C = ctx.shape[1]
    T = S // P
    CT = C // P
    KT = CT + T
    KEYS = C + S
    SH = 16
    SD = D // SH
    SG = 4
    XH = 16
    XD = xwq.shape[1] // XH
    PAIRS = XH // 2
    INNER = XH * XD
    E, _, HID = w1.shape
    HB = HID // P
    NE = E + 1
    assert D == P and XD == 64 and SD == 8 and S == 2 * P and HB == 2

    top = ExitStack()

    def sem(name):
        return top.enter_context(nc.semaphore(name))

    def sb(stack, name, shape, dt=F32):
        return stack.enter_context(nc.sbuf_tensor(name, shape, dt))

    with top:
        ps = top.enter_context(nc.psum_tensor("ps", [P, 8, BANK], F32))

        def slot(s, n=2 * BANK, at=0):
            return ps[:, 2 * s:2 * s + 2, :].rearrange("p a b -> p (a b)")[:, at:at + n]

        ident = sb(top, "ident", [P, P])
        ones = sb(top, "ones", [P, S])
        state = sb(top, "state", [P, B * T, D])
        stats = sb(top, "stats", [P, B * KT, 6])
        mean = sb(top, "mean", [P, B * KT])
        rstd = sb(top, "rstd", [P, B * KT])
        var = sb(top, "var", [P, B * KT])
        tmp = sb(top, "tmp", [P, B * KT])
        gb = sb(top, "gb", [P, 4])
        w_rt = sb(top, "w_rt", [P, E])
        w_up = sb(top, "w_up", [P, 2, NE, HID])
        w_down = sb(top, "w_down", [P, NE, HB, D])

        cross = ExitStack()
        top.enter_context(cross)
        ctx_all = sb(cross, "ctx_all", [P, B * CT, D])
        keep_all = sb(cross, "keep_all", [P, B, C // 4], U32)
        wk_hi = sb(cross, "wk_hi", [P, INNER], F32R)
        wk_lo = sb(cross, "wk_lo", [P, INNER], F32R)
        wv_hi = sb(cross, "wv_hi", [P, INNER], F32R)
        wv_lo = sb(cross, "wv_lo", [P, INNER], F32R)
        wq_hi = sb(cross, "wq_hi", [P, INNER], F32R)
        wq_lo = sb(cross, "wq_lo", [P, INNER], F32R)
        wout = sb(cross, "wout", [P, PAIRS, D])

        m = Shared()
        m.x, m.ctx, m.mask, m.wq, m.wk, m.wv = x, ctx, mask, wq, wk, wv
        m.wo, m.g1, m.b1, m.g2, m.b2, m.xwq = wo, g1, b1, g2, b2, xwq
        m.xwkv, m.xwout, m.w_router, m.w1, m.w3, m.w2 = xwkv, xwout, w_router, w1, w3, w2
        m.sw1, m.sw3, m.sw2, m.B, m.S, m.D = sw1, sw3, sw2, B, S, D
        m.T, m.C, m.CT, m.KT, m.KEYS, m.SH = T, C, CT, KT, KEYS, SH
        m.SD, m.SG, m.XH, m.XD, m.PAIRS, m.INNER = SD, SG, XH, XD, PAIRS, INNER
        m.E, m.NE, m.HID, m.HB, m.ident, m.ones = E, NE, HID, HB, ident, ones
        m.state, m.stats, m.mean, m.rstd, m.gb, m.w_rt = state, stats, mean, rstd, gb, w_rt
        m.ctx_all, m.keep_all, m.wk_hi, m.wk_lo, m.wv_hi, m.wv_lo = ctx_all, keep_all, wk_hi, wk_lo, wv_hi, wv_lo
        m.wq_hi, m.wq_lo, m.wout, m.w_up, m.w_down = wq_hi, wq_lo, wout, w_up, w_down
        m.loaded_up, m.loaded_down = sem("loaded_up"), sem("loaded_down")

        self_attention(nc, sem, sb, ps, m)
        normalize(nc, sem, "n1", B * T, state, stats, mean, rstd, var, tmp, T, CT, KT, whole=True, again=True)
        cross_attention(nc, sem, sb, ps, slot, m)
        normalize(nc, sem, "n2", B * T, state, stats, mean, rstd, var, tmp, T, CT, KT)
        cross.close()
        experts(nc, sem, sb, ps, slot, m)
        normalize(nc, sem, "n3", B * T, state, stats, mean, rstd, var, tmp, T, CT, KT, out=out)


def normalize(nc, sem, name, tiles, state, stats, mean, rstd, var, tmp, T, CT, KT,
              whole=False, again=False, out=None):
    chain = sem(name + "_chain")
    var_ready = sem(name + "_var_ready")
    std_ready = sem(name + "_std_ready")
    bias_ready = sem(name + "_bias_ready")
    act_tiles = sem(name + "_act_tiles")
    stored = sem(name + "_stored")
    rows = stats[:, :, :].rearrange("p (b k) s -> p b k s", k=KT)

    def per_tile(a, everything):
        v = a[:, :].rearrange("p (b k) -> p b k", k=KT)
        return v if everything else v[:, :, CT:KT]

    rounds = [whole] + [False] * again
    with nc.Block() as block:

        @block.vector
        def _(dve):
            count = [0]

            def link(instruction):
                count[0] += 1
                instruction.then_inc(chain, 1)
                dve.wait_ge(chain, count[0])

            def moments(everything):
                st = rows if everything else rows[:, :, CT:KT, :]
                me, ve, mo, vo = (st[:, :, :, i] for i in (1, 2, 4, 5))
                m, v, t = (per_tile(a, everything) for a in (mean, var, tmp))
                link(dve.tensor_tensor(t, me, mo, ALU.subtract))
                link(dve.tensor_tensor(t, t, t, ALU.mult))
                link(dve.tensor_tensor(v, ve, vo, ALU.add))
                link(dve.tensor_scalar(v, v, 1.0 / P, EPS, ALU.mult, ALU.add))
                link(dve.tensor_scalar(t, t, 0.25, None, ALU.mult))
                link(dve.tensor_tensor(m, me, mo, ALU.add))
                link(dve.tensor_scalar(m, m, 0.5, None, ALU.mult))
                dve.tensor_tensor(v, v, t, ALU.add).then_inc(var_ready, 1)

            def reciprocal_root(n, everything):
                v, t, r = (per_tile(a, everything) for a in (var, tmp, rstd))
                dve.wait_ge(std_ready, n)
                link(dve.reciprocal(r, r))
                link(dve.tensor_tensor(t, r, r, ALU.mult))
                link(dve.tensor_tensor(t, t, v, ALU.mult))
                link(dve.tensor_scalar(t, t, -0.5, 1.5, ALU.mult, ALU.add))
                link(dve.tensor_tensor(r, r, t, ALU.mult))

            def at(i):
                return (i // T) * KT + CT + i % T

            for n, everything in enumerate(rounds):
                moments(everything)
                reciprocal_root(n + 1, everything)
                if n == 0:
                    t, m, r = (per_tile(a, False) for a in (tmp, mean, rstd))
                    dve.scalar_tensor_tensor(out=t, in0=m, scalar=-1.0, in1=r,
                                             op0=ALU.mult, op1=ALU.mult).then_inc(bias_ready, 1)
                    for i in range(0, tiles, 2):
                        last = dve.tensor_scalar(state[:, i, :], state[:, i, :], mean[:, at(i):at(i) + 1],
                                                 rstd[:, at(i):at(i) + 1], ALU.subtract, ALU.mult)
                        if out is not None or i == tiles - 2:
                            last.then_inc(chain, 1)
                            count[0] += 1
                    dve.wait_ge(chain, count[0])
                    if again:
                        for i in range(0, tiles, 2):
                            dve.bn_stats(stats[:, at(i), :], state[:, i, :])
                        for i in range(1, tiles, 2):
                            dve.wait_ge(act_tiles, i // 2 + 1)
                            last = dve.bn_stats(stats[:, at(i), :], state[:, i, :])
                        link(last)

        @block.scalar
        def _(act):
            for n, everything in enumerate(rounds):
                act.wait_ge(var_ready, n + 1)
                nc.scalar.activation(per_tile(rstd, everything), per_tile(var, everything),
                                     ACT.Sqrt).then_inc(std_ready, 1)
                if n == 0:
                    act.wait_ge(bias_ready, 1)
                    for i in range(1, tiles, 2):
                        at = (i // T) * KT + CT + i % T
                        nc.scalar.activation(state[:, i, :], state[:, i, :], ACT.Identity, scale=rstd[:, at:at + 1],
                                             bias=tmp[:, at:at + 1]).then_inc(act_tiles, 1)

        if out is not None:
            @block.sync
            def _(sp):
                rows_out = out.rearrange("b (j p) d -> p (b j) d", p=P)
                step = 2 * T
                for i in range(0, tiles, step):
                    sp.wait_ge(chain, 12 + (i + step) // 2)
                    sp.wait_ge(act_tiles, (i + step) // 2)
                    sp.dma_start(rows_out[:, i:i + step, :], state[:, i:i + step, :]).then_inc(stored, 16)
                sp.wait_ge(stored, 16 * (tiles // step))


def self_attention(nc, sem, sb, ps, m):
    B, S, D, T, C, CT, KT = m.B, m.S, m.D, m.T, m.C, m.CT, m.KT
    SH, SD, SG, INNER = m.SH, m.SD, m.SG, m.INNER
    ident, state, stats, gb = m.ident, m.state, m.stats, m.gb
    ctx_all, keep_all, wout, w_rt = m.ctx_all, m.keep_all, m.wout, m.w_rt
    SCALE = float(SD) ** -0.5
    HG = SH // SG
    PV_COLS = 3 * P
    RING = 8
    MASKED = 4
    BANKS = 6

    def bank(s, n=BANK, at=0):
        return ps[:, s, at:at + n]

    mem = ExitStack()
    x_in = sb(mem, "x_in", [P, 2, T, D])
    raw = sb(mem, "raw", [P, 4, D])
    wt = sb(mem, "wt", [P, 3, D])
    wt_hi = sb(mem, "wt_hi", [P, 3, D], F32R)
    wt_lo = sb(mem, "wt_lo", [P, 3, D], F32R)
    aq_hi, aq_lo, ak_hi, ak_lo = (
        sb(mem, n, [P, SG, 4, 32], F32R) for n in ("aq_hi", "aq_lo", "ak_hi", "ak_lo"))
    wo_pad = sb(mem, "wo_pad", [P, SH, 32])
    wo_t = sb(mem, "wo_t", [P, SG, D])
    part = sb(mem, "part", [P, 2])
    head_of = sb(mem, "head_of", [P, HG])
    causal = sb(mem, "causal", [P, S])
    xt_hi = sb(mem, "xt_hi", [P, 2, S], F32R)
    xt_lo = sb(mem, "xt_lo", [P, 2, S], F32R)
    round_kq = sb(mem, "round_kq", [P, 2, S], F32R)
    k_parts = sb(mem, "k_parts", [P, SG, S], F32R)
    q_parts = sb(mem, "q_parts", [P, 2, S], F32R)
    q_head = sb(mem, "q_head", [P, 4, S], F32R)
    vals = sb(mem, "vals", [P, 2, T, SH, 32])
    masked = sb(mem, "masked", [P, MASKED, PV_COLS])
    spare = sb(mem, "spare", [P, MASKED])
    low = sb(mem, "low", [P, MASKED, T])
    probs = sb(mem, "probs", [P, 4, PV_COLS])
    sums = sb(mem, "sums", [P, 2, T, HG])
    rsum = sb(mem, "rsum", [P, 2, T, HG])
    rsum_wide = sb(mem, "rsum_wide", [P, 2, T, HG, 32])
    rsum_t = sb(mem, "rsum_t", [P, 2, S])
    probs_t = sb(mem, "probs_t", [P, RING, PV_COLS])
    heads_t = sb(mem, "heads_t", [P, SG, S])
    raw_kv = sb(mem, "raw_kv", [P, 2 * INNER])
    raw_q = sb(mem, "raw_q", [P, INNER])

    loaded_w, loaded_x, loaded_b = sem("a_loaded_w"), sem("a_loaded_x"), sem("a_loaded_b")
    loaded_kv, loaded_rest = sem("a_loaded_kv"), sem("a_loaded_rest")
    consts = sem("a_consts")
    wt_full = sem("a_wt_full")
    setup = sem("a_setup")
    weights = sem("a_weights")
    cross_hi = sem("a_cross_hi")
    cross_lo = sem("a_cross_lo")
    full = {k: sem(f"a_{k}_full") for k in ("T", "K", "Q", "V", "S", "PT", "R", "OUT")}
    xh_done, x_ready = sem("a_xh_done"), sem("a_x_ready")
    kh_done, k_ready = sem("a_kh_done"), sem("a_k_ready")
    qh_done, q_ready = sem("a_qh_done"), sem("a_q_ready")
    q_head_ready = sem("a_q_head_ready")
    v_ready = sem("a_v_ready")
    masked_ready = sem("a_masked_ready")
    exp_done = sem("a_exp_done")
    pt_act, pt_dve = sem("a_pt_act"), sem("a_pt_dve")
    rsum_ready = sem("a_rsum_ready")
    wide_ready = sem("a_wide_ready")
    rsum_t_ready = sem("a_rsum_t_ready")
    pv_done = sem("a_pv_done")
    heads_ready = sem("a_heads_ready")
    added = sem("a_added")
    measured = sem("a_measured")

    def taken(kind, batch, i):
        if kind == "PT":
            return (pt_dve if i % 2 else pt_act), batch * (SH // 2) + i // 2 + 1
        semaphore, per, steps = {
            "T": (x_ready, 1, 1), "K": (k_ready, SG, 1), "Q": (q_ready, SG, 1), "V": (v_ready, T, 1),
            "S": (masked_ready, SH * T, T), "R": (rsum_t_ready, SG, 1), "OUT": (added, 1, 1)}[kind]
        return semaphore, batch * per + (i + 1) * steps

    pe_order = Order(B, SH, {
        "S": (SH, -0.5), "PT": (SH, 4.75), "K": (SG, -3.5), "Q": (SG, -4), "V": (T, -4),
        "T": (1, -5), "R": (SG, 9.75), "PV": (SG, 9.5), "OUT": (1, 24)})
    dve_order = Order(B, SH, {
        "S": (SH, -0.5), "K": (SG, -3.5), "Q": (SG, -4.25), "PT": (SH // 2, 5.5),
        "XLO": (1, -5.25), "RECIP": (SG, 5.75), "NORM": (SG, 10), "OUT": (1, 23.5),
        "STATS": (1, 28), "V": (T, -4.5)})
    act_order = Order(B, SH, {
        "EXP": (SH, 3), "PT": (SH // 2, 6.75), "K": (SG, -1.75), "Q": (SG, -3), "R": (SG, 11.25),
        "T": (1, -3.5)})
    pool_order = Order(B, SH, {
        "Q_HEAD": (SH, 1.25), "WIDE": (SG, 10.75)})
    banks = Turns(pe_order, full, BANKS)

    x_rows = m.x.rearrange("b (j p) d -> b p j d", p=P)

    with nc.Block() as block:

        @block.sync
        def _(sp):
            for i, w in enumerate((m.wq, m.wk, m.wv, m.wo)):
                sp.dma_start(raw[:, i, :], w).then_inc(loaded_w, 16)

            def load(kind, b, par, i):
                wait(sp, added, b - 1)
                wait(sp, loaded_x, 16 * b)
                sp.dma_start(x_in[:, par, :, :], x_rows[b]).then_inc(loaded_x, 16)
            Order(B, SH, {"LOAD": (1, -SH)}).run(sp, load, 2)
            for n, (shared, routed) in enumerate(((m.sw1, m.w1), (m.sw3, m.w3))):
                sp.dma_start(m.w_up[:, n, 0, :], shared).then_inc(m.loaded_up, 16)
                sp.dma_start(m.w_up[:, n, 1:m.NE, :], routed.rearrange("e d h -> d e h")).then_inc(m.loaded_up, 16)
            sp.dma_start(m.w_down[:, 0, :, :], m.sw2.rearrange("(k p) d -> p k d", p=P)).then_inc(m.loaded_down, 16)
            sp.dma_start(m.w_down[:, 1:m.NE, :, :].rearrange("p e k d -> p (e k) d"),
                         m.w2.rearrange("e (k p) d -> p (e k) d", p=P)).then_inc(m.loaded_down, 16)
            sp.wait_ge(loaded_rest, 16 * 7)

        @block.gpsimd
        def _(pool):
            pool.memset(ident[:, :], 0.0).then_inc(consts, 1)
            pool.memset(causal[:, :], 0.0).then_inc(consts, 1)
            pool.memset(m.ones[:, :], 1.0).then_inc(consts, 1)
            pool.wait_ge(consts, 3)
            pool.affine_select(out=ident[:, :], in_=ident[:, :], compare_op=ALU.not_equal, fill=1.0,
                               base=0, pattern=[[-1, P]], channel_multiplier=1).then_inc(consts, 1)
            pool.affine_select(out=causal[:, P:S], in_=causal[:, P:S], compare_op=ALU.is_ge, fill=BIG,
                               base=0, pattern=[[-1, P]], channel_multiplier=1).then_inc(consts, 1)
            dst = ((m.wk_lo[:, :], raw_kv[:, 0:INNER], m.wk_hi[:, :]),
                   (m.wv_lo[:, :], raw_kv[:, INNER:2 * INNER], m.wv_hi[:, :]),
                   (m.wq_lo[:, :], raw_q[:, :], m.wq_hi[:, :]))
            for i, (lo, whole, hi) in enumerate(dst):
                pool.wait_ge(cross_hi, i + 1)
                pool.tensor_tensor(lo, whole, hi.bitcast(F32), ALU.subtract).then_inc(cross_lo, 1)

            def emit(kind, b, par, i):
                if kind == "Q_HEAD":
                    g = i // HG
                    pool.wait_ge(q_ready, b * SG + g + 1)
                    wait(pool, full["S"], b * SH + i - 3)
                    pool.tensor_tensor(q_head[:, i % 4, :], q_parts[:, g % 2, :].bitcast(F32),
                                       head_of[:, i % HG:i % HG + 1].broadcast_to([P, S]),
                                       ALU.mult).then_inc(q_head_ready, 1)
                if kind == "WIDE":
                    n = b * SG + i
                    wait(pool, full["R"], n - 1)
                    pool.wait_ge(rsum_ready, n + 1)
                    src = rsum[:, i % 2, :, :].rearrange("p t h -> p (t h)").unsqueeze(2)
                    pool.tensor_tensor(rsum_wide[:, i % 2, :, :, :].rearrange("p t h c -> p (t h) c"),
                                       m.ones[:, :].rearrange("p (a c) -> p a c", c=32),
                                       src.broadcast_to([P, T * HG, 32]), ALU.mult).then_inc(wide_ready, 1)
            pool_order.run(pool, emit, 2)

        @block.scalar
        def _(act):
            for w_in, o in ((m.xwkv, raw_kv[:, :]), (m.xwq, raw_q[:, :])):
                act.dma_start(o, w_in).then_inc(loaded_kv, 16)
            for n, w_in in enumerate((m.g1, m.b1, m.g2, m.b2)):
                act.dma_start(gb[:, n:n + 1], w_in.rearrange("(p o) -> p o", o=1)).then_inc(loaded_rest, 16)
            act.dma_start(ctx_all[:, :, :], m.ctx.rearrange("b (j p) d -> p (b j) d", p=P)).then_inc(loaded_b, 16)
            act.dma_start(keep_all[:, :, :], m.mask.rearrange("b c -> (b c)").partition_broadcast(P)
                          .rearrange("p (b c) -> p b c", b=B)).then_inc(loaded_rest, 16)
            act.dma_start(wout[:, :, :], m.xwout.rearrange("(r p) d -> p r d", p=P)).then_inc(loaded_rest, 16)
            act.dma_start(w_rt[:, :], m.w_router).then_inc(loaded_rest, 16)
            act.wait_ge(loaded_kv, 32)
            nc.scalar.activation(m.wk_hi[:, :], raw_kv[:, 0:INNER], ACT.Copy).then_inc(cross_hi, 1)
            nc.scalar.activation(m.wv_hi[:, :], raw_kv[:, INNER:2 * INNER], ACT.Copy).then_inc(cross_hi, 1)
            nc.scalar.activation(m.wq_hi[:, :], raw_q[:, :], ACT.Copy).then_inc(cross_hi, 1)

            def emit(kind, b, par, i):
                if kind == "T":
                    act.wait_ge(full["T"], b + 1)
                    nc.scalar.activation(xt_hi[:, par, :], bank(banks.place("T", 0), S), ACT.Copy).then_inc(xh_done, 1)
                if kind in ("K", "Q"):
                    n, done, read = b * SG + i, *((kh_done, k_ready) if kind == "K" else (qh_done, q_ready))
                    act.wait_ge(full[kind], n + 1)
                    wait(act, read, n)
                    nc.scalar.activation(round_kq[:, "KQ".index(kind), :], bank(banks.place(kind, i), S),
                                         ACT.Copy).then_inc(done, 1)
                if kind == "EXP":
                    n, g = b * SH + i, i // HG
                    wait(act, full["PT"], n - 3)
                    if i % HG == 0:
                        wait(act, rsum_ready, b * SG + g - 1)
                    for j, (lo, hi) in enumerate(((0, P), (P, PV_COLS))):
                        act.wait_ge(masked_ready, T * n + j + 1)
                        r = i % MASKED
                        nc.scalar.activation(probs[:, i % 4, lo:hi], masked[:, r, lo:hi], ACT.Exp,
                                             scale=-1.0, bias=low[:, r, j:j + 1],
                                             accum_out=sums[:, g % 2, j, i % HG:i % HG + 1]).then_inc(exp_done, 1)
                if kind == "PT":
                    g, h = 2 * i // HG, 2 * i
                    act.wait_ge(full["PT"], b * SH + h + 1)
                    wait(act, pv_done, b * SG + g - 1)
                    nc.scalar.activation(probs_t[:, h % RING, :], bank(banks.place("PT", h), PV_COLS),
                                         ACT.Copy).then_inc(pt_act, 1)
                if kind == "R":
                    act.wait_ge(full["R"], b * SG + i + 1)
                    wait(act, heads_ready, b * SG + i - 1)
                    nc.scalar.activation(rsum_t[:, i % 2, :], bank(banks.place("R", i), S), ACT.Copy).then_inc(rsum_t_ready, 1)
            act_order.run(act, emit, 2)

        @block.vector
        def _(dve):
            count = [0]

            def link(instruction):
                count[0] += 1
                instruction.then_inc(setup, 1)
                dve.wait_ge(setup, count[0])

            dve.memset(vals[:, :, :, :, :], 0.0)
            dve.memset(wo_pad[:, :, :], 0.0)
            link(dve.memset(part[:, :], 0.0))
            for rows, col in ((slice(32, 64), 0), (slice(96, 128), 0), (slice(64, 96), 1), (slice(96, 128), 1)):
                last = dve.memset(part[rows, col:col + 1], -1.0)
            link(last)
            dve.wait_ge(consts, 5)
            link(dve.tensor_reduce(head_of[:, :], ident[:, :].rearrange("p (q j c) -> p j q c", q=4, j=HG),
                                   AX.XY, ALU.add))
            dve.wait_ge(loaded_w, 64)
            link(dve.tensor_copy(wo_pad[:, :, 0:SD], raw[:, 3, :].rearrange("p (h c) -> p h c", h=SH)))
            dve.wait_ge(wt_full, 1)
            dve.tensor_scalar(wt[:, 0, :], bank(0, P), -SCALE, None, ALU.mult)
            link(dve.tensor_copy(wt[:, 1:3, :].rearrange("p a b -> p (a b)"), bank(0, 2 * P, P)))
            link(dve.tensor_copy(wt_hi[:, :, :], wt[:, :, :]))
            link(dve.tensor_tensor(wt_lo[:, :, :], wt[:, :, :], wt_hi[:, :, :].bitcast(F32), ALU.subtract))
            for hi, lo, n in ((aq_hi, aq_lo, 0), (ak_hi, ak_lo, 1)):
                for dst, src in ((hi, wt_hi), (lo, wt_lo)):
                    last = dve.tensor_copy(dst[:, :, :, :], src[:, n, :].bitcast(F32).rearrange("p (g c) -> p g c", g=SG)
                                           .unsqueeze(2).broadcast_to([P, SG, 4, 32]))
            last.then_inc(weights, 1)
            dve.wait_ge(wt_full, 2)
            dve.tensor_copy(wo_t[:, :, :].rearrange("p g d -> p (g d)"), bank(2, SG * D)).then_inc(weights, 1)
            dve.wait_ge(loaded_b, 16)

            def emit(kind, b, par, i):
                if kind == "V":
                    dve.wait_ge(full["V"], b * T + i + 1)
                    wait(dve, pv_done, (b - 1) * SG + 1)
                    dve.tensor_copy(vals[:, par, i, :, 0:SD],
                                    bank(banks.place("V", i), D).rearrange("p (h c) -> p h c", h=SH)).then_inc(v_ready, 1)
                if kind == "XLO":
                    dve.wait_ge(xh_done, b + 1)
                    dve.tensor_tensor(xt_lo[:, par, :], bank(banks.place("T", 0), S),
                                      xt_hi[:, par, :].bitcast(F32), ALU.subtract).then_inc(x_ready, 1)
                if kind == "K":
                    dve.wait_ge(kh_done, b * SG + i + 1)
                    wait(dve, full["S"], (b - 1) * SH + HG * (i + 1))
                    dve.scalar_tensor_tensor(out=k_parts[:, i, :], in0=round_kq[:, 0, :].bitcast(F32),
                                             scalar=part[:, 0:1], in1=bank(banks.place("K", i), S),
                                             op0=ALU.mult, op1=ALU.add).then_inc(k_ready, 1)
                if kind == "Q":
                    dve.wait_ge(qh_done, b * SG + i + 1)
                    wait(dve, q_head_ready, b * SH + HG * (i - 1))
                    dve.scalar_tensor_tensor(out=q_parts[:, i % 2, :], in0=round_kq[:, 1, :].bitcast(F32),
                                             scalar=part[:, 1:2], in1=bank(banks.place("Q", i), S),
                                             op0=ALU.mult, op1=ALU.add).then_inc(q_ready, 1)
                if kind == "S":
                    n, s, r = b * SH + i, banks.place("S", i), i % MASKED
                    dve.wait_ge(consts, 5)
                    dve.wait_ge(full["S"], n + 1)
                    wait(dve, exp_done, T * (n + 1 - MASKED))
                    hold(dve, spare[:, r:r + 1])
                    for j, (lo, hi) in enumerate(((0, P), (P, PV_COLS))):
                        dve.tensor_tensor_reduce(masked[:, r, lo:hi], bank(s, hi - lo, j * S),
                                                 causal[:, S - (hi - lo):S], 1.0, 3e38, ALU.add, ALU.min,
                                                 low[:, r, j:j + 1]).then_inc(masked_ready, 1)
                if kind == "PT":
                    g, h = 2 * i // HG, 2 * i + 1
                    dve.wait_ge(full["PT"], b * SH + h + 1)
                    wait(dve, pv_done, b * SG + g - 1)
                    dve.tensor_copy(probs_t[:, h % RING, :], bank(banks.place("PT", h), PV_COLS)).then_inc(pt_dve, 1)
                if kind == "RECIP":
                    n = b * SG + i
                    dve.wait_ge(exp_done, T * HG * (n + 1))
                    wait(dve, wide_ready, n - 1)
                    dve.reciprocal(rsum[:, i % 2, :, :], sums[:, i % 2, :, :]).then_inc(rsum_ready, 1)
                if kind == "NORM":
                    n = b * SG + i
                    dve.wait_ge(rsum_t_ready, n + 1)
                    dve.wait_ge(pv_done, n + 1)
                    if i == 0:
                        wait(dve, full["OUT"], b)
                    dve.tensor_tensor(heads_t[:, i, :], ps[:, O_BANK + i % 2, 0:S], rsum_t[:, i % 2, :],
                                      ALU.mult).then_inc(heads_ready, 1)
                if kind == "OUT":
                    dve.wait_ge(full["OUT"], b + 1)
                    dve.tensor_tensor(state[:, bass.ds(b * T, T), :],
                                      bank(banks.place("OUT", 0), T * D).rearrange("p (t d) -> p t d", t=T),
                                      x_in[:, par, :, :], ALU.add).then_inc(added, 1)
                if kind == "STATS":
                    for j in range(CT):
                        dve.bn_stats(stats[:, bass.ds(b * KT + j, 1), :], ctx_all[:, bass.ds(b * CT + j, 1), :])
                    dve.wait_ge(added, b + 1)
                    for j in range(T):
                        last = dve.bn_stats(stats[:, bass.ds(b * KT + CT + j, 1), :], state[:, bass.ds(b * T + j, 1), :])
                    last.then_inc(measured, 1)
            dve_order.run(dve, emit, 2)

        @block.tensor
        def _(pe):
            pe.wait_ge(consts, 4)
            pe.wait_ge(loaded_w, 64)
            for i in range(3):
                last = nc.tensor.transpose(bank(0, P, i * P), raw[:, i, :], ident[:, :])
            last.then_inc(wt_full, 1)
            pe.wait_ge(setup, 4)
            for g in range(SG):
                last = nc.tensor.transpose(bank(2, P, g * P),
                                           wo_pad[:, 4 * g:4 * g + 4, :].rearrange("p h c -> p (h c)"), ident[:, :])
            last.then_inc(wt_full, 1)
            def emit(kind, b, par, i):
                if kind in full:
                    s = banks.place(kind, i)
                    earlier = banks.before(kind, b, i)
                    if earlier:
                        wait(pe, *taken(*earlier))
                if kind == "T":
                    pe.wait_ge(loaded_x, 16 * (b + 1))
                    for j in range(T):
                        last = nc.tensor.transpose(bank(s, P, j * P), x_in[:, par, j, :], ident[:, :])
                    last.then_inc(full["T"], 1)
                if kind in ("K", "Q", "V"):
                    pe.wait_ge(weights, 1)
                    pe.wait_ge(x_ready, b + 1)
                if kind in ("K", "Q"):
                    wh, wl = (a[:, i, :, :].rearrange("p r c -> p (r c)")
                              for a in ((ak_hi, ak_lo) if kind == "K" else (aq_hi, aq_lo)))
                    nc.tensor.matmul(bank(s, S), wh, xt_hi[:, par, :], start=True, stop=False)
                    nc.tensor.matmul(bank(s, S), wh, xt_lo[:, par, :], start=False, stop=False)
                    nc.tensor.matmul(bank(s, S), wl, xt_hi[:, par, :], start=False, stop=True).then_inc(full[kind], 1)
                if kind == "V":
                    wh, wl = wt_hi[:, 2, :], wt_lo[:, 2, :]
                    xh, xl = (a[:, par, i * P:(i + 1) * P] for a in (xt_hi, xt_lo))
                    nc.tensor.matmul(bank(s, D), xh, wh, start=True, stop=False)
                    nc.tensor.matmul(bank(s, D), xh, wl, start=False, stop=False)
                    nc.tensor.matmul(bank(s, D), xl, wh, start=False, stop=True).then_inc(full["V"], 1)
                if kind == "S":
                    pe.wait_ge(k_ready, b * SG + i // HG + 1)
                    pe.wait_ge(q_head_ready, b * SH + i + 1)
                    for j in range(T):
                        last = nc.tensor.matmul(bank(s, S, j * S), q_head[:, i % 4, j * P:(j + 1) * P],
                                                k_parts[:, i // HG, :], start=True, stop=True)
                    last.then_inc(full["S"], 1)
                if kind == "PT":
                    pe.wait_ge(exp_done, T * (b * SH + i + 1))
                    for j in range(3):
                        last = nc.tensor.transpose(bank(s, P, j * P), probs[:, i % 4, j * P:(j + 1) * P], ident[:, :])
                    last.then_inc(full["PT"], 1)
                if kind == "PV":
                    n = b * SG + i
                    pe.wait_ge(pt_act, (n + 1) * HG // 2)
                    pe.wait_ge(pt_dve, (n + 1) * HG // 2)
                    pe.wait_ge(v_ready, T * (b + 1))
                    wait(pe, heads_ready, n - 1)
                    for kt, lo in ((0, 0), (1, P)):
                        for j in range(HG):
                            h = i * HG + j
                            last = nc.tensor.matmul(ps[32 * j:32 * j + 32, O_BANK + i % 2, lo:S],
                                                    vals[:, par, kt, h, :],
                                                    probs_t[:, h % RING, kt * S:kt * S + S - lo],
                                                    start=(kt == 0), stop=(kt == 1), skip_group_check=True)
                    last.then_inc(pv_done, 1)
                if kind == "R":
                    pe.wait_ge(wide_ready, b * SG + i + 1)
                    for j in range(T):
                        last = nc.tensor.transpose(bank(s, P, j * P),
                                                   rsum_wide[:, i % 2, j, :, :].rearrange("p h c -> p (h c)"), ident[:, :])
                    last.then_inc(full["R"], 1)
                if kind == "OUT":
                    pe.wait_ge(weights, 2)
                    pe.wait_ge(heads_ready, SG * (b + 1))
                    for j in range(T):
                        for g in range(SG):
                            last = nc.tensor.matmul(bank(s, D, j * D), heads_t[:, g, j * P:(j + 1) * P], wo_t[:, g, :],
                                                    start=(g == 0), stop=(g == SG - 1))
                    last.then_inc(full["OUT"], 1)
            pe_order.run(pe, emit, 2)
    mem.close()


def cross_attention(nc, sem, sb, ps, slot, m):
    B, S, D, T, C, CT, KT, KEYS = m.B, m.S, m.D, m.T, m.C, m.CT, m.KT, m.KEYS
    XH, XD, PAIRS = m.XH, m.XD, m.PAIRS
    ident, state, stats, mean, rstd, gb = m.ident, m.state, m.stats, m.mean, m.rstd, m.gb
    UNITS = XH * T
    Q_SCALE = -float(XD) ** -0.5

    mem = ExitStack()
    bar = sb(mem, "bar", [P, 2, KEYS])
    normed = sb(mem, "normed", [P, KT, D])
    y = sb(mem, "y", [P, KEYS])
    k_raw = sb(mem, "k_raw", [P, KEYS])
    y_hi = sb(mem, "y_hi", [P, 2, KEYS], F32R)
    y_lo = sb(mem, "y_lo", [P, 2, KEYS], F32R)
    vals = sb(mem, "xvals", [P, 2, KT, 4 * XD])
    k_parts = sb(mem, "xk_parts", [P, 2, 2, KEYS], F32R)
    q_parts = sb(mem, "xq_parts", [P, 2, 2, 2, S], F32R)
    masked = sb(mem, "xmasked", [P, 4, KEYS])
    spare = sb(mem, "xspare", [P, 4])
    low = sb(mem, "xlow", [P, 4])
    probs = sb(mem, "xprobs", [P, 4, KEYS])
    sums = sb(mem, "xsums", [P, 4, 2, T])
    rsum = sb(mem, "xrsum", [P, 2, 2, T])
    rsum_wide = sb(mem, "xrsum_wide", [P, 2, T, 2, XD])
    rsum_t = sb(mem, "xrsum_t", [P, 2, S])
    probs_t = sb(mem, "xprobs_t", [P, 4, KT, T, P])
    heads_t = sb(mem, "xheads_t", [P, PAIRS, S])

    bar_zeroed = sem("x_bar_zeroed")
    bar_ready = sem("x_bar_ready")
    normed_ready = sem("x_normed_ready")
    full = {k: sem(f"x_{k}_full") for k in ("TC", "TX", "K", "Q", "V", "S", "PT", "R", "OUT")}
    yc_ready, yx_ready = sem("x_yc_ready"), sem("x_yx_ready")
    yh_done, y_split = sem("x_yh_done"), sem("x_y_split")
    k_out = sem("x_k_out")
    kh_done, k_ready = sem("x_kh_done"), sem("x_k_ready")
    q_hi_done, q_lo_done = sem("x_q_hi_done"), sem("x_q_lo_done")
    q_ready = sem("x_q_ready")
    v_ready = sem("x_v_ready")
    masked_ready = sem("x_masked_ready")
    exp_done = sem("x_exp_done")
    pt_act, pt_dve = sem("x_pt_act"), sem("x_pt_dve")
    rsum_ready = sem("x_rsum_ready")
    wide_ready = sem("x_wide_ready")
    rsum_t_ready = sem("x_rsum_t_ready")
    pv_done = sem("x_pv_done")
    heads_ready = sem("x_heads_ready")
    added = sem("x_added")
    measured = sem("x_measured")

    def taken(kind, batch, i):
        if kind == "PT":
            return (pt_dve if i % 2 else pt_act), batch * (UNITS // 2) + i // 2 + 1
        if kind == "Q":
            return q_lo_done, batch * XH + 2 * i + 2
        semaphore, per = {
            "TC": (yc_ready, 1), "TX": (yx_ready, 1), "K": (k_out, PAIRS), "V": (v_ready, PAIRS),
            "S": (masked_ready, UNITS), "R": (rsum_t_ready, PAIRS), "OUT": (added, 1)}[kind]
        return semaphore, batch * per + i + 1

    pe_order = Order(B, UNITS, {
        "S": (UNITS, -2.25), "K": (PAIRS, -5.75), "Q": (PAIRS, -7.25), "V": (PAIRS, -4),
        "R": (PAIRS, 5.25), "PV": (PAIRS, 5), "PT": (UNITS, 0.75), "OUT": (1, 37.75),
        "TC": (1, -23), "TX": (1, -26)})
    dve_order = Order(B, UNITS, {
        "S": (UNITS, -1.75), "Q": (PAIRS, -6), "HI": (XH, -4), "RECIP": (PAIRS, 2.5),
        "NORM": (PAIRS, 9.25), "PT": (UNITS // 2, 2.25), "OUT": (1, 38.5), "NORMED": (1, -26.75),
        "BAR": (1, -26), "Y": (1, -19), "TWICE": (XH, -5)})
    act_order = Order(B, UNITS, {
        "K": (PAIRS, -5), "Q": (PAIRS, -6.75), "V": (PAIRS, -3.25), "R": (PAIRS, 5.5),
        "PT": (UNITS // 2, 1.25), "EXP": (UNITS, -1), "TC": (1, -22.75), "TX": (1, -26)})
    pool_order = Order(B, UNITS, {
        "LO": (XH, -17.5), "WIDE": (PAIRS, -9.25), "Y": (1, -25)})
    slots = Turns(pe_order, full, SLOTS)

    with nc.Block() as block:

        @block.gpsimd
        def _(pool):
            turns = Turns(pool_order, ("LO", "Y", "WIDE"), 1)

            def finished(kind, batch, i):
                semaphore, per = {"LO": (k_ready, XH), "Y": (y_split, 1), "WIDE": (wide_ready, PAIRS)}[kind]
                return semaphore, batch * per + i + 1

            def emit(kind, b, par, i):
                earlier = turns.before(kind, b, i)
                if earlier:
                    wait(pool, *finished(*earlier))
                if kind == "LO":
                    n, h = b * XH + i, i % 2
                    dst, src = ((slice(XD, P), slice(0, XD)), (slice(0, XD), slice(XD, P)))[h]
                    pool.wait_ge(kh_done, n + 1)
                    pool.tensor_tensor(k_parts[dst, i // 2 % 2, h, :], k_raw[src, :],
                                       k_parts[src, i // 2 % 2, h, :].bitcast(F32), ALU.subtract).then_inc(k_ready, 1)
                if kind == "Y":
                    pool.wait_ge(yh_done, b + 1)
                    pool.tensor_tensor(y_lo[:, par, :], y[:, :], y_hi[:, par, :].bitcast(F32),
                                       ALU.subtract).then_inc(y_split, 1)
                if kind == "WIDE":
                    n = b * PAIRS + i
                    pool.wait_ge(rsum_ready, n + 1)
                    wait(pool, full["R"], n - 1)
                    for j in range(T):
                        last = pool.tensor_tensor(rsum_wide[:, i % 2, j, :, :],
                                                  m.ones[:, 0:P].rearrange("p (a c) -> p a c", c=XD),
                                                  rsum[:, i % 2, :, j:j + 1].broadcast_to([P, 2, XD]), ALU.mult)
                    last.then_inc(wide_ready, 1)
            pool_order.run(pool, emit, 2)

        @block.scalar
        def _(act):
            def emit(kind, b, par, i):
                if kind in ("TC", "TX"):
                    act.wait_ge(full[kind], b + 1)
                    wait(act, y_split, b)
                    lo, hi, g, ready = {"TC": (0, C, 0, yc_ready), "TX": (C, KEYS, 2, yx_ready)}[kind]
                    nc.scalar.activation(y[:, lo:hi], slot(slots.place(kind, 0), hi - lo), ACT.Identity,
                                         scale=gb[:, g:g + 1], bias=gb[:, g + 1:g + 2]).then_inc(ready, 1)
                if kind == "K":
                    act.wait_ge(full["K"], b * PAIRS + i + 1)
                    wait(act, k_ready, b * XH + 2 * i)
                    nc.scalar.activation(k_raw[:, :], slot(slots.place("K", i), KEYS), ACT.Copy).then_inc(k_out, 1)
                if kind == "Q":
                    act.wait_ge(full["Q"], b * PAIRS + i + 1)
                    wait(act, full["S"], b * UNITS + 4 * (i - 1))
                    for h in range(2):
                        rows = slice(h * XD, (h + 1) * XD)
                        nc.scalar.activation(q_parts[rows, i % 2, h, 0, :], slot(slots.place("Q", i), S)[rows, :],
                                             ACT.Copy, scale=Q_SCALE).then_inc(q_hi_done, 1)
                if kind == "V":
                    act.wait_ge(full["V"], b * PAIRS + i + 1)
                    wait(act, pv_done, b * PAIRS + i // 2 * 2 - 2)
                    half = slice(i % 2 * (KT // 2), (i % 2 + 1) * (KT // 2))
                    nc.scalar.activation(vals[:, i // 2 % 2, half, :].rearrange("p k c -> p (k c)"),
                                         slot(slots.place("V", i), KT // 2 * 4 * XD), ACT.Copy).then_inc(v_ready, 1)
                if kind == "EXP":
                    pair, n = i // 4, b * UNITS + i
                    wait(act, full["PT"], n - 3)
                    if i % 4 == 0:
                        wait(act, rsum_ready, b * PAIRS + pair - 3)
                    act.wait_ge(masked_ready, n + 1)
                    nc.scalar.activation(probs[:, i % 4, :], masked[:, i % 4, :], ACT.Exp, scale=-1.0,
                                         bias=low[:, i % 4:i % 4 + 1],
                                         accum_out=sums[:, pair % 4, i // 2 % 2, i % 2:i % 2 + 1]).then_inc(exp_done, 1)
                if kind == "PT":
                    act.wait_ge(full["PT"], b * UNITS + 2 * i + 1)
                    wait(act, pv_done, b * PAIRS + i // 2 - 1)
                    nc.scalar.activation(probs_t[:, i % 4, :, 0, :],
                                         slot(slots.place("PT", 2 * i), KEYS).rearrange("p (k t) -> p k t", k=KT),
                                         ACT.Copy).then_inc(pt_act, 1)
                if kind == "R":
                    act.wait_ge(full["R"], b * PAIRS + i + 1)
                    wait(act, heads_ready, b * PAIRS + i - 1)
                    nc.scalar.activation(rsum_t[:, i % 2, :], slot(slots.place("R", i), S), ACT.Copy).then_inc(rsum_t_ready, 1)
            act_order.run(act, emit, 2)

        @block.vector
        def _(dve):
            dve.memset(bar[:, :, C:KEYS], 0.0).then_inc(bar_zeroed, 1)

            def emit(kind, b, par, i):
                if kind == "NORMED":
                    wait(dve, full["TX"], b)
                    wait(dve, full["TC"], b)
                    for j in range(KT):
                        src = (m.ctx_all[:, bass.ds(b * CT + j, 1), :] if j < CT
                               else state[:, bass.ds(b * T + j - CT, 1), :])
                        last = dve.tensor_scalar(normed[:, j:j + 1, :], src, mean[:, bass.ds(b * KT + j, 1)],
                                                 rstd[:, bass.ds(b * KT + j, 1)], ALU.subtract, ALU.mult)
                    last.then_inc(normed_ready, 1)
                if kind == "BAR":
                    wait(dve, masked_ready, (b - 1) * UNITS)
                    dve.tensor_scalar(bar[:, par:par + 1, 0:C], m.keep_all[:, bass.ds(b, 1), :].bitcast(U8), -BIG, BIG,
                                      ALU.mult, ALU.add).then_inc(bar_ready, 1)
                if kind == "Y":
                    dve.wait_ge(yc_ready, b + 1)
                    dve.wait_ge(yx_ready, b + 1)
                    dve.tensor_copy(y_hi[:, par, :], y[:, :]).then_inc(yh_done, 1)
                if kind == "HI":
                    n, h = b * XH + i, i % 2
                    rows = slice(h * XD, (h + 1) * XD)
                    dve.wait_ge(k_out, b * PAIRS + i // 2 + 1)
                    wait(dve, full["S"], 2 * n - 6)
                    dve.tensor_copy(k_parts[rows, i // 2 % 2, h, :], k_raw[rows, :]).then_inc(kh_done, 1)
                if kind == "Q":
                    for h in range(2):
                        rows = slice(h * XD, (h + 1) * XD)
                        dve.wait_ge(q_hi_done, b * XH + 2 * i + h + 1)
                        dve.scalar_tensor_tensor(out=q_parts[rows, i % 2, h, 1, :],
                                                 in0=slot(slots.place("Q", i), S)[rows, :], scalar=Q_SCALE,
                                                 in1=q_parts[rows, i % 2, h, 0, :].bitcast(F32),
                                                 op0=ALU.mult, op1=ALU.subtract).then_inc(q_lo_done, 1)
                if kind == "TWICE":
                    n, h = b * XH + i, i % 2
                    src, dst = (slice(0, XD), slice(XD, P)) if h == 0 else (slice(XD, P), slice(0, XD))
                    dve.wait_ge(q_lo_done, n + 1)
                    wait(dve, full["S"], 2 * n - 6)
                    dve.tensor_copy(q_parts[dst, i // 2 % 2, h, :, :],
                                    q_parts[src, i // 2 % 2, h, :, :].bitcast(F32)).then_inc(q_ready, 1)
                if kind == "S":
                    n = b * UNITS + i
                    dve.wait_ge(bar_zeroed, 1)
                    if i == 0:
                        dve.wait_ge(bar_ready, b + 1)
                    dve.wait_ge(full["S"], n + 1)
                    wait(dve, exp_done, n - 3)
                    hold(dve, spare[:, i % 4:i % 4 + 1])
                    dve.tensor_tensor_reduce(masked[:, i % 4, :], slot(slots.place("S", i), KEYS), bar[:, par, :], 1.0, 3e38,
                                             ALU.add, ALU.min, low[:, i % 4:i % 4 + 1]).then_inc(masked_ready, 1)
                if kind == "PT":
                    dve.wait_ge(full["PT"], b * UNITS + 2 * i + 2)
                    wait(dve, pv_done, b * PAIRS + i // 2 - 1)
                    dve.tensor_copy(probs_t[:, i % 4, :, 1, :],
                                    slot(slots.place("PT", 2 * i + 1), KEYS).rearrange("p (k t) -> p k t", k=KT)
                                    ).then_inc(pt_dve, 1)
                if kind == "RECIP":
                    n = b * PAIRS + i
                    dve.wait_ge(exp_done, 4 * (n + 1))
                    wait(dve, wide_ready, n - 1)
                    dve.reciprocal(rsum[:, i % 2, :, :], sums[:, i % 4, :, :]).then_inc(rsum_ready, 1)
                if kind == "NORM":
                    n = b * PAIRS + i
                    dve.wait_ge(rsum_t_ready, n + 1)
                    dve.wait_ge(pv_done, n + 1)
                    if i == 0:
                        wait(dve, full["OUT"], b)
                    dve.tensor_tensor(heads_t[:, i, :], ps[:, O_BANK + i % 2, 0:S], rsum_t[:, i % 2, :],
                                      ALU.mult).then_inc(heads_ready, 1)
                if kind == "OUT":
                    dve.wait_ge(full["OUT"], b + 1)
                    tokens = state[:, bass.ds(b * T, T), :]
                    dve.tensor_tensor(tokens, slot(slots.place("OUT", 0), T * D).rearrange("p (t d) -> p t d", t=T), tokens,
                                      ALU.add).then_inc(added, 1)
                    dve.wait_ge(added, b + 1)
                    for j in range(T):
                        last = dve.bn_stats(stats[:, bass.ds(b * KT + CT + j, 1), :], state[:, bass.ds(b * T + j, 1), :])
                    last.then_inc(measured, 1)
            dve_order.run(dve, emit, 2)

        @block.tensor
        def _(pe):
            wk_hi, wk_lo, wv_hi, wv_lo = m.wk_hi, m.wk_lo, m.wv_hi, m.wv_lo

            def emit(kind, b, par, i):
                if kind in full:
                    s = slots.place(kind, i)
                    earlier = slots.before(kind, b, i)
                    if earlier:
                        wait(pe, *taken(*earlier))
                if kind in ("TC", "TX"):
                    pe.wait_ge(normed_ready, b + 1)
                    for n, j in enumerate(range(CT) if kind == "TC" else range(CT, KT)):
                        last = nc.tensor.transpose(slot(s, P, n * P), normed[:, j, :], ident[:, :])
                    last.then_inc(full[kind], 1)
                if kind == "K":
                    pe.wait_ge(y_split, b + 1)
                    wh, wl = (a[:, i * P:(i + 1) * P] for a in (wk_hi, wk_lo))
                    for lo, hi in ((0, C), (C, KEYS)):
                        o = slot(s, hi - lo, lo)
                        nc.tensor.matmul(o, wh, y_hi[:, par, lo:hi], start=True, stop=False)
                        nc.tensor.matmul(o, wh, y_lo[:, par, lo:hi], start=False, stop=False)
                        last = nc.tensor.matmul(o, wl, y_hi[:, par, lo:hi], start=False, stop=True)
                    last.then_inc(full["K"], 1)
                if kind == "Q":
                    pe.wait_ge(y_split, b + 1)
                    wh, wl = (a[:, i * P:(i + 1) * P] for a in (m.wq_hi, m.wq_lo))
                    nc.tensor.matmul(slot(s, S), wh, y_hi[:, par, C:KEYS], start=True, stop=False)
                    nc.tensor.matmul(slot(s, S), wh, y_lo[:, par, C:KEYS], start=False, stop=False)
                    nc.tensor.matmul(slot(s, S), wl, y_hi[:, par, C:KEYS], start=False, stop=True
                                     ).then_inc(full["Q"], 1)
                if kind == "V":
                    pe.wait_ge(y_split, b + 1)
                    cols = slice(i // 2 * 4 * XD, (i // 2 + 1) * 4 * XD)
                    for n in range(KT // 2):
                        j = i % 2 * (KT // 2) + n
                        yh, yl = (a[:, par, j * P:(j + 1) * P] for a in (y_hi, y_lo))
                        o = slot(s, 4 * XD, n * 4 * XD)
                        nc.tensor.matmul(o, yh, wv_hi[:, cols], start=True, stop=False)
                        nc.tensor.matmul(o, yh, wv_lo[:, cols], start=False, stop=False)
                        last = nc.tensor.matmul(o, yl, wv_hi[:, cols], start=False, stop=True)
                    last.then_inc(full["V"], 1)
                if kind == "S":
                    pair, h, t = i // 4, i // 2 % 2, i % 2
                    pe.wait_ge(k_ready, b * XH + 2 * pair + h + 1)
                    pe.wait_ge(q_ready, b * XH + 2 * pair + h + 1)
                    for lo, hi in ((0, C), (C, KEYS)):
                        for part in range(2):
                            last = nc.tensor.matmul(slot(s, hi - lo, lo), q_parts[:, pair % 2, h, part, t * P:(t + 1) * P],
                                                    k_parts[:, pair % 2, h, lo:hi], start=part == 0, stop=part == 1)
                    last.then_inc(full["S"], 1)
                if kind == "PT":
                    pe.wait_ge(exp_done, b * UNITS + i + 1)
                    for j in range(KT):
                        last = nc.tensor.transpose(slot(s, P, j * P), probs[:, i % 4, j * P:(j + 1) * P], ident[:, :])
                    last.then_inc(full["PT"], 1)
                if kind == "PV":
                    n = b * PAIRS + i
                    pe.wait_ge(pt_act, 2 * (n + 1))
                    pe.wait_ge(pt_dve, 2 * (n + 1))
                    pe.wait_ge(v_ready, b * PAIRS + i // 2 * 2 + 2)
                    wait(pe, heads_ready, n - 1)
                    for j in range(KT):
                        for h in range(2):
                            c = (i % 2 * 2 + h) * XD
                            last = nc.tensor.matmul(ps[h * XD:(h + 1) * XD, O_BANK + i % 2, 0:S],
                                                    vals[:, i // 2 % 2, j, c:c + XD],
                                                    probs_t[:, (2 * i + h) % 4, j, :, :].rearrange("p t q -> p (t q)"),
                                                    start=(j == 0), stop=(j == KT - 1), skip_group_check=True)
                    last.then_inc(pv_done, 1)
                if kind == "R":
                    pe.wait_ge(wide_ready, b * PAIRS + i + 1)
                    for j in range(T):
                        last = nc.tensor.transpose(slot(s, P, j * P),
                                                   rsum_wide[:, i % 2, j, :, :].rearrange("p h c -> p (h c)"), ident[:, :])
                    last.then_inc(full["R"], 1)
                if kind == "OUT":
                    pe.wait_ge(heads_ready, PAIRS * (b + 1))
                    for t in range(T):
                        for pair in range(PAIRS):
                            last = nc.tensor.matmul(slot(s, D, t * D), heads_t[:, pair, t * P:(t + 1) * P],
                                                    m.wout[:, pair, :], start=(pair == 0), stop=(pair == PAIRS - 1))
                    last.then_inc(full["OUT"], 1)
            pe_order.run(pe, emit, 2)
    mem.close()


def experts(nc, sem, sb, ps, slot, m):
    B, S, D, T, CT, KT, E, NE, HID, HB = m.B, m.S, m.D, m.T, m.CT, m.KT, m.E, m.NE, m.HID, m.HB
    ident, state, stats, w_rt, w_up, w_down = m.ident, m.state, m.stats, m.w_rt, m.w_up, m.w_down
    TILES = B * T

    mem = ExitStack()
    up_hi = sb(mem, "up_hi", [P, 2, NE, HID], F32R)
    up_lo = sb(mem, "up_lo", [P, 2, NE, HID], F32R)
    xt = sb(mem, "xt", [P, TILES * P])
    xt_hi = sb(mem, "cxt_hi", [P, TILES * P], F32R)
    xt_lo = sb(mem, "cxt_lo", [P, TILES * P], F32R)
    logits = sb(mem, "logits", [P, TILES, E])
    index = sb(mem, "index", [P, TILES, E])
    best = sb(mem, "best", [P, 2, TILES])
    first = sb(mem, "first", [P, TILES])
    chosen = sb(mem, "chosen", [P, 2, TILES, E])
    scratch = sb(mem, "scratch", [P, TILES, E])
    gap = sb(mem, "gap", [P, TILES])
    gate = sb(mem, "gate", [P, 2, TILES])
    gates = sb(mem, "gates", [P, TILES, E])
    silu = sb(mem, "silu", [P, 3, HB * S])
    hidden = sb(mem, "hidden", [P, 3, HB * S])

    index_ready = sem("e_index_ready")
    up_hi_done, up_ready = sem("e_up_hi_done"), sem("e_up_ready")
    xt_full, xt_copied = sem("e_xt_full"), sem("e_xt_copied")
    xh_done, x_ready = sem("e_xh_done"), sem("e_x_ready")
    logits_full = sem("e_logits_full")
    chain = sem("e_chain")
    gap_ready, exp_gap = sem("e_gap_ready"), sem("e_exp_gap")
    gates_ready = sem("e_gates_ready")
    full = {k: sem(f"e_{k}_full") for k in ("H", "Y")}
    silu_done = sem("e_silu_done")
    hidden_ready = sem("e_hidden_ready")
    summed = sem("e_summed")
    measured = sem("e_measured")

    def taken(kind, batch, i):
        if kind == "H":
            return hidden_ready, batch * NE + i + 1
        return summed, (batch * NE + i + 1) * T

    LAG = 2
    order = Order(B, NE, {"H": (NE, 0), "Y": (NE, LAG)})
    slots = Turns(order, full, SLOTS)

    with nc.Block() as block:

        @block.gpsimd
        def _(pool):
            for e in range(E):
                last = pool.memset(index[:, :, e:e + 1], float(e - E))
            last.then_inc(index_ready, 1)
            for e in range(NE):
                pool.wait_ge(up_hi_done, e + 1)
                pool.tensor_tensor(up_lo[:, :, e, :], w_up[:, :, e, :], up_hi[:, :, e, :].bitcast(F32),
                                   ALU.subtract).then_inc(up_ready, 1)

        @block.scalar
        def _(act):
            act.wait_ge(m.loaded_up, 64)
            for e in range(2):
                nc.scalar.activation(up_hi[:, :, e, :], w_up[:, :, e, :], ACT.Copy).then_inc(up_hi_done, 1)
            for n in range(TILES // 8):
                act.wait_ge(xt_full, n + 1)
                nc.scalar.activation(xt[:, n * 8 * P:(n + 1) * 8 * P], slot(n), ACT.Copy).then_inc(xt_copied, 1)
            for e in range(2, NE):
                nc.scalar.activation(up_hi[:, :, e, :], w_up[:, :, e, :], ACT.Copy).then_inc(up_hi_done, 1)
            act.wait_ge(gap_ready, 1)
            nc.scalar.activation(gap[:, :], gap[:, :], ACT.Exp).then_inc(exp_gap, 1)

            def emit(kind, b, par, i):
                if kind == "H":
                    n, s = b * NE + i, slots.place(kind, i)
                    act.wait_ge(full["H"], n + 1)
                    wait(act, hidden_ready, n - 2)
                    nc.scalar.activation(silu[:, i % 3, :],
                                         slot(s, HB * S), ACT.Silu).then_inc(silu_done, 1)
            order.run(act, emit, 1)

        @block.vector
        def _(dve):
            count = [0]

            def link(instruction):
                count[0] += 1
                instruction.then_inc(chain, 1)
                dve.wait_ge(chain, count[0])

            for n in range(TILES // 8):
                cols = slice(n * 8 * P, (n + 1) * 8 * P)
                dve.wait_ge(xt_copied, n + 1)
                dve.tensor_copy(xt_hi[:, cols], xt[:, cols]).then_inc(xh_done, 1)
                dve.wait_ge(xh_done, n + 1)
                dve.tensor_tensor(xt_lo[:, cols], xt[:, cols], xt_hi[:, cols].bitcast(F32), ALU.subtract).then_inc(x_ready, 1)
            dve.wait_ge(logits_full, 1)
            link(dve.tensor_copy(logits[:, :, :], ps[:, O_BANK, 0:TILES * E].rearrange("p (t e) -> p t e", e=E)))
            dve.wait_ge(index_ready, 1)
            for n in range(2):
                top, pick = best[:, n, :], chosen[:, n, :, :]
                link(dve.tensor_reduce(top, logits[:, :, :], AX.X, ALU.max))
                link(dve.tensor_tensor(scratch[:, :, :], logits[:, :, :], top.unsqueeze(2).broadcast_to([P, TILES, E]),
                                       ALU.is_equal))
                link(dve.tensor_tensor(scratch[:, :, :], scratch[:, :, :], index[:, :, :], ALU.mult))
                link(dve.tensor_reduce(first[:, :], scratch[:, :, :], AX.X, ALU.min))
                link(dve.tensor_tensor(pick, index[:, :, :], first[:, :].unsqueeze(2).broadcast_to([P, TILES, E]),
                                       ALU.is_equal))
                if n == 0:
                    link(dve.scalar_tensor_tensor(out=logits[:, :, :], in0=pick, scalar=-3e38, in1=logits[:, :, :],
                                                  op0=ALU.mult, op1=ALU.add))
            dve.tensor_tensor(gap[:, :], best[:, 1, :], best[:, 0, :], ALU.subtract).then_inc(gap_ready, 1)
            dve.wait_ge(exp_gap, 1)
            link(dve.tensor_scalar(gate[:, 0, :], gap[:, :], 1.0, None, ALU.add))
            link(dve.reciprocal(gate[:, 0, :], gate[:, 0, :]))
            link(dve.tensor_tensor(gate[:, 1, :], gate[:, 0, :], gap[:, :], ALU.mult))
            for n in range(2):
                link(dve.tensor_tensor(chosen[:, n, :, :], chosen[:, n, :, :],
                                       gate[:, n, :].unsqueeze(2).broadcast_to([P, TILES, E]), ALU.mult))
            dve.tensor_tensor(gates[:, :, :], chosen[:, 0, :, :], chosen[:, 1, :, :], ALU.add).then_inc(gates_ready, 1)
            dve.wait_ge(gates_ready, 1)

            def emit(kind, b, par, i):
                n, s = b * NE + i, slots.place(kind, i)
                if kind == "H":
                    dve.wait_ge(silu_done, n + 1)
                    wait(dve, full["Y"], n - 2)
                    dve.tensor_tensor(hidden[:, i % 3, :], slot(s, HB * S, BANK),
                                      silu[:, i % 3, :], ALU.mult).then_inc(hidden_ready, 1)
                if kind == "Y":
                    dve.wait_ge(full["Y"], n + 1)
                    for j in range(T):
                        tokens = state[:, bass.ds(b * T + j, 1), :]
                        y = slot(s, D, j * D).unsqueeze(1)
                        wait(dve, summed, n * T + j - 1)
                        if i == 0:
                            dve.tensor_tensor(tokens, y, tokens, ALU.add).then_inc(summed, 1)
                        else:
                            at = gates[:, bass.ds(b * T + j, 1), i - 1:i].rearrange("p a b -> p (a b)")
                            dve.scalar_tensor_tensor(out=tokens, in0=y, scalar=at, in1=tokens,
                                                     op0=ALU.mult, op1=ALU.add).then_inc(summed, 1)
                    if i == NE - 1:
                        dve.wait_ge(summed, (n + 1) * T)
                        for j in range(T):
                            last = dve.bn_stats(stats[:, bass.ds(b * KT + CT + j, 1), :], state[:, bass.ds(b * T + j, 1), :])
                        last.then_inc(measured, 1)
            order.run(dve, emit, 1)

        @block.tensor
        def _(pe):
            for n in range(TILES // 8):
                for j in range(8):
                    last = nc.tensor.transpose(slot(n, P, j * P), state[:, 8 * n + j, :], ident[:, :])
                last.then_inc(xt_full, 1)
            for i in range(TILES):
                if i % 8 == 0:
                    pe.wait_ge(xt_copied, i // 8 + 1)
                last = nc.tensor.matmul(ps[:, O_BANK, i * E:(i + 1) * E], xt[:, i * P:(i + 1) * P], w_rt[:, :], start=True, stop=True)
            last.then_inc(logits_full, 1)
            pe.wait_ge(m.loaded_down, 32)

            def emit(kind, b, par, i):
                n, s = b * NE + i, slots.place(kind, i)
                earlier = slots.before(kind, b, i)
                if earlier:
                    wait(pe, *taken(*earlier))
                if kind == "H":
                    first_batch = isinstance(b, int) and b == 0
                    pe.wait_ge(x_ready, 1 if first_batch else TILES // 8)
                    pe.wait_ge(up_ready, i + 1 if first_batch else NE)
                    xh, xl = (a[:, bass.ds(b * S, S)] for a in (xt_hi, xt_lo))
                    for part in range(2):
                        for k in range(HB):
                            o = slot(s, S, part * BANK + k * S)
                            wh, wl = (a[:, part, i, k * P:(k + 1) * P] for a in (up_hi, up_lo))
                            nc.tensor.matmul(o, wh, xh, start=True, stop=False)
                            nc.tensor.matmul(o, wh, xl, start=False, stop=False)
                            last = nc.tensor.matmul(o, wl, xh, start=False, stop=True)
                    last.then_inc(full["H"], 1)
                if kind == "Y":
                    pe.wait_ge(hidden_ready, n + 1)
                    for j in range(T):
                        for k in range(HB):
                            last = nc.tensor.matmul(slot(s, D, j * D),
                                                    hidden[:, i % 3, k * S + j * P:k * S + (j + 1) * P],
                                                    w_down[:, i, k, :], start=(k == 0), stop=(k == HB - 1))
                    last.then_inc(full["Y"], 1)
            order.run(pe, emit, 1)
    mem.close()


INPUTS = ["x", "ctx_1024", "mask_BxS2_bk0", "L0_attn_q_proj_weight", "L0_attn_k_proj_weight",
          "L0_attn_v_proj_weight", "L0_attn_o_proj_weight", "L0_xattn_g1", "L0_xattn_b1", "L0_xattn_g2",
          "L0_xattn_b2", "L0_xattn_Wq", "L0_xattn_Wkv", "L0_xattn_Wout", "L0_ffn_w_router", "L0_ffn_w1",
          "L0_ffn_w3", "L0_ffn_w2", "L0_ffn_sw1", "L0_ffn_sw3", "L0_ffn_sw2"]


def kernel(**inputs):
    import numpy as np
    from concourse import bacc
    from concourse.bass_utils import run_bass_kernel_spmd

    nc = bacc.Bacc("TRN2", target_bir_lowering=False, num_devices=1)
    arrays, args = {}, []
    for name in INPUTS:
        a = np.ascontiguousarray(inputs[name])
        if a.dtype == np.bool_:
            a = a.view(np.uint32)
        arrays[f"in_{name}"] = a
        args.append(nc.dram_tensor(f"in_{name}", a.shape, mybir.dt.from_np(a.dtype), kind="ExternalInput").ap())
    out = nc.dram_tensor("out", inputs["x"].shape, F32, kind="ExternalOutput").ap()
    decoder_layer(nc, *args, out)
    return run_bass_kernel_spmd(nc, [arrays], core_ids=[0]).results[0]["out"]
```
